# Optimizing a Trainium2 kernel written in Bass

```python
import numpy as np
import jax
import jax.numpy as jnp

def _softmax(x, axis=-1):
    return jax.nn.softmax(x, axis=axis)

def _gelu(x):
    return jax.nn.gelu(x, approximate=True)

def _silu(x):
    return jax.nn.silu(x)

def _sigmoid(x):
    return jax.nn.sigmoid(x)

def _layernorm(x, axis=-1, eps=1e-05):
    m = jnp.mean(x, axis=axis, keepdims=True)
    v = jnp.var(x, axis=axis, keepdims=True)
    return (x - m) / jnp.sqrt(v + eps)

def _scatter_add(tgt, idx, src, axis=0):
    return tgt.at[idx].add(src)

def _segment_sum(src, seg, n):
    return jax.ops.segment_sum(src, seg, n)
kernel_name = 'mk_lm_tower_d1_tok_ids768_r4_869e9a'

def setup_inputs(seed: int=0):
    np.random.seed(seed)
    _w = jnp.asarray

    def _rec_inputs():
        import jax
        import jax.numpy as jnp
        _rk = jax.random.key(seed)
        x = jax.random.randint(jax.random.fold_in(_rk, 1), (2, 1024), 0, 31999, jnp.int32)
        mask_BS_i2_0 = jnp.where(jnp.ones((2, 1024), dtype=bool), 2, 0).astype(jnp.int32)
        return (x, mask_BS_i2_0)
    x, mask_BS_i2_0 = _rec_inputs()

    def _L0_tok_setup():
        import jax, jax.numpy as jnp
        import numpy as np
        VOCAB = 8000
        DIM = 192
        BATCH = 8
        SEQ = 512

        def _sinusoidal_pos(seq_len, dim):
            pos = jnp.arange(seq_len, dtype=jnp.float32)[:, None]
            ids = jnp.arange(dim, dtype=jnp.float32)[None, :]
            even_exp = jnp.floor(ids / 2.0) * 2.0 / dim
            angle = pos / jnp.power(10000.0, even_exp)
            return jnp.where(jnp.arange(dim) % 2 == 0, jnp.sin(angle), jnp.cos(angle))
        key = jax.random.key(seed)
        k1, k2, k3, k4 = jax.random.split(key, 4)
        input_tensor = jax.random.randint(k1, (BATCH, SEQ), 0, VOCAB)
        segment_label = jax.random.randint(k2, (BATCH, SEQ), 0, 3)
        token_table = jax.random.normal(k3, (VOCAB, DIM), dtype=jnp.float32) * 0.02
        segm_table = jax.random.normal(k4, (3, DIM), dtype=jnp.float32) * 0.02
        token_table = token_table.at[0].set(0.0)
        segm_table = segm_table.at[0].set(0.0)
        return {'input_tensor': input_tensor, 'segment_label': segment_label, 'token_table': token_table, 'segm_table': segm_table}
    _L0_tok_all = _L0_tok_setup()
    _L0_tok_in = {k: v for k, v in _L0_tok_all.items() if k in ('token_table', 'segm_table')}
    del _L0_tok_all

    def _L0_attn_setup():
        import jax, jax.numpy as jnp
        import numpy as np
        NUM_HEADS = 12
        BITS_W = 8
        BITS_A = 8
        BITS_S = 4
        EPS = 1.1920928955078125e-07

        def fq_weight(w):
            qmin, qmax = (-2 ** (BITS_W - 1), 2 ** (BITS_W - 1) - 1)
            mn = jnp.minimum(w.min(axis=1, keepdims=True), 0.0)
            mx = jnp.maximum(w.max(axis=1, keepdims=True), 0.0)
            scale = jnp.maximum((mx - mn) / float(qmax - qmin), EPS)
            zp = qmin - jnp.round(mn / scale)
            wq = jnp.clip(jnp.round(w / scale) + zp, qmin, qmax)
            return (wq - zp) * scale

        def fq_act(x):
            qmin, qmax = (-2 ** (BITS_A - 1), 2 ** (BITS_A - 1) - 1)
            mn = jnp.minimum(x.min(), 0.0)
            mx = jnp.maximum(x.max(), 0.0)
            scale = jnp.maximum((mx - mn) / float(qmax - qmin), EPS)
            zp = qmin - jnp.round(mn / scale)
            xq = jnp.clip(jnp.round(x / scale) + zp, qmin, qmax)
            return ((xq - zp) * scale, scale)

        def int_log_softmax(x, scale):
            x_int = x / scale
            x_int = x_int - x_int.max(axis=-1, keepdims=True)
            x0, n = (-0.6931, 30)
            x0_int = jnp.floor(x0 / scale)
            x_int = jnp.maximum(x_int, n * x0_int)
            q = jnp.floor(x_int / x0_int)
            r = x_int - x0_int * q
            c0 = 0.35815147
            b_int = jnp.floor(0.96963238 / c0 / scale)
            c_int = jnp.floor(1.0 / c0 / (scale * scale))
            z = r * (r + b_int) + c_int
            exp_int = jnp.clip(jnp.floor(z * jnp.exp2(n - q)), 0.0, None)
            exp_sum = exp_int.sum(axis=-1, keepdims=True)
            sm = jnp.round(exp_sum / exp_int)
            big = jnp.floor(jnp.log2(sm))
            big = jnp.where(sm - jnp.exp2(big) >= jnp.exp2(big - 1.0), big + 1.0, big)
            mask = big >= float(2 ** BITS_S)
            qlog = jnp.clip(big, 0.0, float(2 ** BITS_S - 1))
            return jnp.where(mask, 0.0, jnp.exp2(-qlog))
        key = jax.random.key(seed)
        ks = jax.random.split(key, 5)
        B, N, C = (16, 577, 192)
        return {'x': jax.random.normal(ks[0], (B, N, C), jnp.float32), 'w_qkv': jax.random.normal(ks[1], (3 * C, C), jnp.float32) * 0.02, 'b_qkv': jax.random.normal(ks[2], (3 * C,), jnp.float32) * 0.02, 'w_proj': jax.random.normal(ks[3], (C, C), jnp.float32) * 0.02, 'b_proj': jax.random.normal(ks[4], (C,), jnp.float32) * 0.02}
    _L0_attn_all = _L0_attn_setup()
    _L0_attn_in = {k: v for k, v in _L0_attn_all.items() if k in ('w_qkv', 'b_qkv', 'w_proj', 'b_proj')}
    del _L0_attn_all

    def _L0_ffn_setup():
        import jax, jax.numpy as jnp
        import numpy as np
        TOP_K = 2
        key = jax.random.key(seed)
        ks = jax.random.split(key, 5)
        B, S, D, H, E = (1, 512, 192, 768, 8)
        x = jax.random.normal(ks[0], (B, S, D), dtype=jnp.float32)
        gate_w = jax.random.normal(ks[1], (E, D), dtype=jnp.float32) * 0.02
        w1 = jax.random.normal(ks[2], (E, D, H), dtype=jnp.float32) * 0.02
        b1 = jnp.zeros((E, H), dtype=jnp.float32)
        w2 = jax.random.normal(ks[3], (E, H, D), dtype=jnp.float32) * 0.02
        b2 = jnp.zeros((E, D), dtype=jnp.float32)
        return {'x': x, 'gate_w': gate_w, 'w1': w1, 'b1': b1, 'w2': w2, 'b2': b2}
    _L0_ffn_all = _L0_ffn_setup()
    _L0_ffn_in = {k: v for k, v in _L0_ffn_all.items() if k in ('gate_w', 'w1', 'b1', 'w2', 'b2')}
    del _L0_ffn_all
    return {'x': x, 'mask_BS_i2_0': mask_BS_i2_0, 'L0_tok_token_table': _L0_tok_in['token_table'], 'L0_tok_segm_table': _L0_tok_in['segm_table'], 'L0_attn_w_qkv': _L0_attn_in['w_qkv'], 'L0_attn_b_qkv': _L0_attn_in['b_qkv'], 'L0_attn_w_proj': _L0_attn_in['w_proj'], 'L0_attn_b_proj': _L0_attn_in['b_proj'], 'L0_ffn_gate_w': _L0_ffn_in['gate_w'], 'L0_ffn_w1': _L0_ffn_in['w1'], 'L0_ffn_b1': _L0_ffn_in['b1'], 'L0_ffn_w2': _L0_ffn_in['w2'], 'L0_ffn_b2': _L0_ffn_in['b2']}

def reference(x, mask_BS_i2_0, L0_tok_token_table, L0_tok_segm_table, L0_attn_w_qkv, L0_attn_b_qkv, L0_attn_w_proj, L0_attn_b_proj, L0_ffn_gate_w, L0_ffn_w1, L0_ffn_b1, L0_ffn_w2, L0_ffn_b2):
    import jax
    import jax.numpy as jnp

    def _L0_tok_ref(input_tensor, segment_label, token_table, segm_table):
        import jax, jax.numpy as jnp
        import numpy as np
        VOCAB = 8000
        DIM = 192
        BATCH = 8
        SEQ = 512

        def _sinusoidal_pos(seq_len, dim):
            pos = jnp.arange(seq_len, dtype=jnp.float32)[:, None]
            ids = jnp.arange(dim, dtype=jnp.float32)[None, :]
            even_exp = jnp.floor(ids / 2.0) * 2.0 / dim
            angle = pos / jnp.power(10000.0, even_exp)
            return jnp.where(jnp.arange(dim) % 2 == 0, jnp.sin(angle), jnp.cos(angle))
        batch, seq = input_tensor.shape
        pos = _sinusoidal_pos(seq, token_table.shape[1])
        tokens_embed = token_table[input_tensor]
        segments_embed = segm_table[segment_label]
        return segments_embed + pos[None, :, :] + tokens_embed

    def _L0_attn_ref(x, w_qkv, b_qkv, w_proj, b_proj):
        import jax, jax.numpy as jnp
        import numpy as np
        NUM_HEADS = 12
        BITS_W = 8
        BITS_A = 8
        BITS_S = 4
        EPS = 1.1920928955078125e-07

        def fq_weight(w):
            qmin, qmax = (-2 ** (BITS_W - 1), 2 ** (BITS_W - 1) - 1)
            mn = jnp.minimum(w.min(axis=1, keepdims=True), 0.0)
            mx = jnp.maximum(w.max(axis=1, keepdims=True), 0.0)
            scale = jnp.maximum((mx - mn) / float(qmax - qmin), EPS)
            zp = qmin - jnp.round(mn / scale)
            wq = jnp.clip(jnp.round(w / scale) + zp, qmin, qmax)
            return (wq - zp) * scale

        def fq_act(x):
            qmin, qmax = (-2 ** (BITS_A - 1), 2 ** (BITS_A - 1) - 1)
            mn = jnp.minimum(x.min(), 0.0)
            mx = jnp.maximum(x.max(), 0.0)
            scale = jnp.maximum((mx - mn) / float(qmax - qmin), EPS)
            zp = qmin - jnp.round(mn / scale)
            xq = jnp.clip(jnp.round(x / scale) + zp, qmin, qmax)
            return ((xq - zp) * scale, scale)

        def int_log_softmax(x, scale):
            x_int = x / scale
            x_int = x_int - x_int.max(axis=-1, keepdims=True)
            x0, n = (-0.6931, 30)
            x0_int = jnp.floor(x0 / scale)
            x_int = jnp.maximum(x_int, n * x0_int)
            q = jnp.floor(x_int / x0_int)
            r = x_int - x0_int * q
            c0 = 0.35815147
            b_int = jnp.floor(0.96963238 / c0 / scale)
            c_int = jnp.floor(1.0 / c0 / (scale * scale))
            z = r * (r + b_int) + c_int
            exp_int = jnp.clip(jnp.floor(z * jnp.exp2(n - q)), 0.0, None)
            exp_sum = exp_int.sum(axis=-1, keepdims=True)
            sm = jnp.round(exp_sum / exp_int)
            big = jnp.floor(jnp.log2(sm))
            big = jnp.where(sm - jnp.exp2(big) >= jnp.exp2(big - 1.0), big + 1.0, big)
            mask = big >= float(2 ** BITS_S)
            qlog = jnp.clip(big, 0.0, float(2 ** BITS_S - 1))
            return jnp.where(mask, 0.0, jnp.exp2(-qlog))
        B, N, C = x.shape
        H = NUM_HEADS
        hd = C // H
        attn_scale = hd ** (-0.5)
        y = x @ fq_weight(w_qkv).T + b_qkv
        y, _ = fq_act(y)
        qkv = y.reshape(B, N, 3, H, hd).transpose(2, 0, 3, 1, 4)
        q, k, v = (qkv[0], qkv[1], qkv[2])
        attn = jnp.einsum('bhnd,bhmd->bhnm', q, k) * attn_scale
        attn, s_attn = fq_act(attn)
        attn = int_log_softmax(attn, s_attn)
        o = jnp.einsum('bhnm,bhmd->bhnd', attn, v)
        o = o.transpose(0, 2, 1, 3).reshape(B, N, C)
        o, _ = fq_act(o)
        o = o @ fq_weight(w_proj).T + b_proj
        o, _ = fq_act(o)
        return o

    def _L0_ffn_ref(x, gate_w, w1, b1, w2, b2):
        import jax, jax.numpy as jnp
        import numpy as np
        TOP_K = 2
        B, S, D = x.shape
        E, _, H = w1.shape
        T = B * S
        K = TOP_K
        xf = x.reshape(T, D)
        logits = xf @ gate_w.T
        probs = jax.nn.softmax(logits, axis=-1)
        top_w, top_i = jax.lax.top_k(probs, K)
        top_w = top_w / (jnp.sum(top_w, axis=-1, keepdims=True) + 1e-09)
        flat_e = top_i.reshape(-1)
        flat_w = top_w.reshape(-1)
        tok_idx = jnp.repeat(jnp.arange(T), K)
        order = jnp.argsort(flat_e)
        se = flat_e[order]
        pt = tok_idx[order]
        pw = flat_w[order]
        counts = jax.ops.segment_sum(jnp.ones(T * K, jnp.int32), se, num_segments=E)
        starts = jnp.concatenate([jnp.zeros((1,), jnp.int32), jnp.cumsum(counts)[:-1]])
        pos = jnp.arange(T * K) - starts[se]
        cap = T * K
        padded = jnp.zeros((E, cap, D), x.dtype).at[se, pos].set(xf[pt])
        hidden = jax.nn.gelu(jnp.einsum('ecd,edh->ech', padded, w1) + b1[:, None, :], approximate=False)
        out = jnp.einsum('ech,ehd->ecd', hidden, w2) + b2[:, None, :]
        expert_out = out[se, pos] * pw[:, None]
        final = jnp.zeros((T, D), x.dtype).at[pt].add(expert_out)
        return final.reshape(B, S, D)
    h = _L0_tok_ref(x, mask_BS_i2_0, L0_tok_token_table, L0_tok_segm_table)
    h = h + _L0_attn_ref(_layernorm(h, axis=-1), L0_attn_w_qkv, L0_attn_b_qkv, L0_attn_w_proj, L0_attn_b_proj)
    h = h + _L0_ffn_ref(_layernorm(h, axis=-1), L0_ffn_gate_w, L0_ffn_w1, L0_ffn_b1, L0_ffn_w2, L0_ffn_b2)
    return h

_drawn_inputs = setup_inputs


def setup_inputs(seed=0):
    import zlib

    import numpy as np

    out = dict(_drawn_inputs(seed))
    spreads = {'L0_ffn_b1': (0.0, 0.1), 'L0_ffn_b2': (0.0, 0.1)}
    factors = {'L0_attn_b_qkv': 4.761}
    for name, (base, spread) in spreads.items():
        noise = np.random.default_rng([zlib.crc32(name.encode()), seed]).standard_normal(out[name].shape)
        drawn = base * np.exp(spread * noise) if base else spread * noise
        out[name] = jnp.asarray(drawn.astype(out[name].dtype))
    for name, factor in factors.items():
        out[name] = (out[name] * factor).astype(out[name].dtype)
    return out
```

```python
from contextlib import ExitStack

import concourse.bass as bass
from concourse import mybir



ALU = mybir.AluOpType
ACT = mybir.ActivationFunctionType
F32 = mybir.dt.float32
BF16 = mybir.dt.bfloat16
I16 = mybir.dt.int16
U16 = mybir.dt.uint16
I32 = mybir.dt.int32
U32 = mybir.dt.uint32
AX = mybir.AxisListType.X
RMAX = bass.bass_isa.ReduceOp.max

P = 128
B, S = 2, 1024
TOK = B * S
NT = TOK // P
TB = S // P
D = 192
KC = 2
KP = D // KC
HEADS, HD = 12, 16
HPC = P // HD
NG = 4
GT = NT // NG
GTOK = GT * P
WCH = 6
VOCAB, SEGS = 8000, 3
E, H = 8, 768
HC = H // P

ROUND = 12582912.0
EPS_SCALE = 1.1920928955078125e-07
LN_EPS = 1e-05
QMAX = 255.0

X0 = 0.6931
C0 = 0.35815147
B_NUM = 0.96963238 / C0
C_NUM = 1.0 / C0
N_HALVINGS = 30.0
POW2 = 4.0 / 3.0 * (1.0 - 2.0 ** -9) * (1.0 + 1e-6)
EXP_MASK = 0x7F80
PSHIFT = 111


class Norm:

    def __init__(self, sb, sem, name):
        self.stats = sb(name + "_stats", [P, NT, 6], F32)
        self.meanvar = sb(name + "_meanvar", [P, NT, 2], F32)
        self.vareps = sb(name + "_vareps", [P, NT], F32)
        self.root = sb(name + "_root", [P, NT], F32)
        self.tmp = sb(name + "_tmp", [P, NT], F32)
        self.rstd = sb(name + "_rstd", [P, NT], F32)
        self.stats_done = sem(name + "_stats_done")
        self.aggr_done = sem(name + "_aggr_done")
        self.var_ready = sem(name + "_var_ready")
        self.root_ready = sem(name + "_root_ready")
        self.normed = sem(name + "_normed")


def layer_norm_dve(nc, dve, L, src, dst, g, n):
    lo, hi = n * g, n * g + n
    for r in range(lo, hi):
        nc.vector.bn_stats(L.stats[:, r, :], src[:, r, :]).then_inc(L.stats_done, 1)
    for r in range(lo, hi):
        dve.wait_ge(L.stats_done, r + 1)
        nc.vector.bn_aggr(L.meanvar[:, r, :], L.stats[:, r, :]).then_inc(L.aggr_done, 1)
    dve.wait_ge(L.aggr_done, hi)
    var, root = L.vareps[:, lo:hi], L.root[:, lo:hi]
    nc.vector.tensor_scalar(var, L.meanvar[:, lo:hi, 1], LN_EPS, None, ALU.add).then_inc(L.var_ready, 1)
    dve.wait_ge(L.root_ready, g + 1)
    step = L.chain
    step(nc.vector.reciprocal(L.tmp[:, lo:hi], root))
    step(nc.vector.tensor_tensor(L.tmp[:, lo:hi], L.tmp[:, lo:hi], var, ALU.mult))
    step(nc.vector.scalar_tensor_tensor(out=L.tmp[:, lo:hi], in0=L.tmp[:, lo:hi], scalar=0.0, in1=root,
                                        op0=ALU.add, op1=ALU.add))
    step(nc.vector.tensor_scalar(L.tmp[:, lo:hi], L.tmp[:, lo:hi], 0.5, None, ALU.mult))
    step(nc.vector.reciprocal(L.rstd[:, lo:hi], L.tmp[:, lo:hi]))
    for r in range(lo, hi):
        nc.vector.tensor_scalar(dst[:, r, :], src[:, r, :], L.meanvar[:, r, 0:1], L.rstd[:, r:r + 1],
                                ALU.subtract, ALU.mult).then_inc(L.normed, 1)


def layer_norm_act(nc, act, L, g, n):
    act.wait_ge(L.var_ready, g + 1)
    nc.scalar.activation(L.root[:, n * g:n * g + n], L.vareps[:, n * g:n * g + n], ACT.Sqrt).then_inc(L.root_ready, 1)


def chain_on(eng, sem):
    count = [0]

    def step(ins):
        count[0] += 1
        ins.then_inc(sem, 1)
        eng.wait_ge(sem, count[0])

    return step


def quant_params_dve(nc, step, ext, pr):
    scale, inv, low, high = (pr[:, i:i + 1] for i in range(4))
    step(nc.vector.tensor_scalar(ext, ext, 0.0, None, ALU.max))
    step(nc.vector.tensor_tensor(scale, ext[:, 0:1], ext[:, 1:2], ALU.add))
    step(nc.vector.tensor_scalar(scale, scale, 1.0 / QMAX, EPS_SCALE, ALU.mult, ALU.max))
    step(nc.vector.reciprocal(inv, scale))
    step(nc.vector.tensor_scalar(low, ext[:, 1:2], inv, ROUND, ALU.mult, ALU.add))
    step(nc.vector.tensor_scalar(low, low, ROUND, -1.0, ALU.subtract, ALU.mult))
    step(nc.vector.tensor_scalar(high, low, QMAX, None, ALU.add))


class Inputs:
    pass


class Shared:
    pass


def load_weights_and_tokens(nc, t, io):
    with ExitStack() as ctx:
        def sb(name, shape, dt):
            return ctx.enter_context(nc.sbuf_tensor(name, shape, dt))

        def sem(name):
            return ctx.enter_context(nc.semaphore(name))

        ids = sb("ids", [P, 2, NT], I32)
        idf = sb("idf", [P, 2, NT], F32)
        wrap = sb("wrap", [P, 2, NT], F32)
        rows = sb("rows", [P, 2, NT], U32)
        tok_rows = sb("tok_rows", [P, NT, D], F32)
        seg_rows = sb("seg_rows", [P, NT, D], F32)
        pos = sb("pos_sb", [P, TB, D], F32)
        xn = tok_rows
        xT = sb("xT", [KP, KC, TOK], F32)
        wraw = sb("wraw", [P, WCH + 2, D], F32)
        wint = sb("wint", [P, WCH + 2, D], BF16)
        wext = sb("wext", [P, 6, WCH + 2], F32)
        wT = sb("wT", [KP, KC, WCH, P], F32)
        bias = sb("bias", [P, WCH], F32)
        y = sb("y", [P, WCH, TOK], F32)
        yext = sb("yext", [P, 2, NG, WCH], F32)
        ymm = sb("ymm", [P, 2], F32)
        vint = seg_rows[:].rearrange("p r d -> p (r d)")[:, 0:TOK].bitcast(BF16).rearrange(
            "p (c n) -> p c n", c=2)
        psT = ctx.enter_context(nc.psum_tensor("psT", [P, 2, 512], F32))
        psW = ctx.enter_context(nc.psum_tensor("psW", [P, 2, 1024], BF16))
        psY = ctx.enter_context(nc.psum_tensor("psY", [P, 4, 512], F32))

        L = Norm(sb, sem, "norm1")
        ids_in, w_in, pos_in, const_in, bias_in = (sem(n) for n in ("ids_in", "w_in", "pos_in", "const_in", "bias_in"))
        pad_ready, rows_ready, dve_step = sem("pad_ready"), sem("rows_ready"), sem("dve_step")
        gathered = [sem(f"gathered{g}") for g in range(NG)]
        wint_ready, wT_ps, wT_ready = sem("wint_ready"), sem("wT_ps"), sem("wT_ready")
        xT_ps, xT_ready, y_ps, y_ready, y_ext = (sem(n) for n in ("xT_ps", "xT_ready", "y_ps", "y_ready", "y_ext"))
        ymm_ready, ymm_all, vint_ready, v_ps, v_ready = (
            sem(n) for n in ("ymm_ready", "ymm_all", "vint_ready", "v_ps", "v_ready"))
        sum_done, h_ready = sem("sum_done"), sem("h_ready")
        n_w_loads = WCH + 2

        block = ctx.enter_context(nc.Block())

        @block.sync
        def _(sp):
            with nc.allow_non_contiguous_dma("token ids"):
                for i, src in enumerate((io.x, io.mask)):
                    sp.dma_start(ids[:, i, :], src.rearrange("b s -> (b s)").rearrange("(r p) -> p r", p=P)).then_inc(ids_in, 16)
            sp.wait_ge(pad_ready, 1)
            for part in range(4):
                src, r0 = (io.w_qkv, part * D) if part < 3 else (io.w_proj, 0)
                sp.dma_start(wraw[:, 2 * part, :], src[r0:r0 + P, :]).then_inc(w_in, 16)
                sp.dma_start(wraw[0:D - P, 2 * part + 1, :], src[r0 + P:r0 + D, :]).then_inc(w_in, 16)
            sp.dma_start(pos[:], io.pos.rearrange("(r p) d -> p r d", p=P)).then_inc(pos_in, 16)
            sp.dma_start(t.ident[:], io.ident).then_inc(const_in, 16)
            sp.dma_start(t.headmask[:], io.headmask).then_inc(const_in, 16)
            sp.wait_ge(pad_ready, 2)
            with nc.allow_non_contiguous_dma("one bias per partition"):
                for part in range(3):
                    r0 = part * D
                    sp.dma_start(bias[:, 2 * part:2 * part + 1], io.b_qkv[r0:r0 + P].unsqueeze(1)).then_inc(bias_in, 16)
                    sp.dma_start(bias[0:D - P, 2 * part + 1:2 * part + 2],
                                 io.b_qkv[r0 + P:r0 + D].unsqueeze(1)).then_inc(bias_in, 16)

        @block.gpsimd
        def _(pool):
            nc.gpsimd.memset(wraw[:], 0.0).then_inc(pad_ready, 1)
            nc.gpsimd.memset(bias[:], 0.0).then_inc(pad_ready, 1)
            pool.wait_ge(rows_ready, 2)
            for g in range(NG):
                for r in range(g * GT, g * GT + GT):
                    for i, (dst, table) in enumerate(((tok_rows, io.token_table), (seg_rows, io.segm_table))):
                        pool.indirect_dma_start(
                            out=dst[:, r, :], out_offset=None, in_=table,
                            in_offset=bass.IndirectOffsetOnAxis(ap=rows[:, i, r:r + 1], axis=0),
                        ).then_inc(gathered[g], 16)
            pool.wait_ge(ymm_ready, 2)
            nc.gpsimd.partition_all_reduce(t.yall[:], ymm[:], P, RMAX).then_inc(ymm_all, 1)

        @block.vector
        def _(dve):
            step = L.chain = chain_on(dve, dve_step)
            dve.wait_ge(ids_in, 32)
            for i, n in enumerate((VOCAB, SEGS)):
                step(nc.vector.tensor_scalar(wrap[:, i, :], ids[:, i, :], 0.0, float(n), ALU.is_lt, ALU.mult))
                step(nc.vector.tensor_tensor(idf[:, i, :], wrap[:, i, :], ids[:, i, :], ALU.add))
                nc.vector.tensor_scalar(rows[:, i, :], idf[:, i, :], 0.0, float(n - 1), ALU.max, ALU.min).then_inc(rows_ready, 1)
            dve.wait_ge(w_in, 16 * n_w_loads)
            mx, nmn, sc, inv, low, high = (wext[:, i, :] for i in range(6))
            step(nc.vector.tensor_reduce(mx, wraw[:], AX, ALU.max))
            step(nc.vector.tensor_reduce(nmn, wraw[:], AX, ALU.min, negate=True))
            step(nc.vector.tensor_scalar(wext[:, 0:2, :], wext[:, 0:2, :], 0.0, None, ALU.max))
            step(nc.vector.tensor_tensor(sc, mx, nmn, ALU.add))
            step(nc.vector.tensor_scalar(t.wscale[:], sc, 1.0 / QMAX, EPS_SCALE, ALU.mult, ALU.max))
            step(nc.vector.reciprocal(inv, t.wscale[:]))
            step(nc.vector.tensor_tensor(low, nmn, inv, ALU.mult))
            step(nc.vector.tensor_scalar(low, low, ROUND, ROUND, ALU.add, ALU.subtract))
            step(nc.vector.tensor_scalar(low, low, -1.0, None, ALU.mult))
            step(nc.vector.tensor_scalar(high, low, QMAX, None, ALU.add))
            for c in range(WCH + 2):
                step(nc.vector.tensor_scalar(wraw[:, c, :], wraw[:, c, :], inv[:, c:c + 1], ROUND, ALU.mult, ALU.add))
                step(nc.vector.tensor_scalar(wraw[:, c, :], wraw[:, c, :], ROUND, low[:, c:c + 1], ALU.subtract, ALU.max))
                nc.vector.tensor_scalar(wint[:, c, :], wraw[:, c, :], high[:, c:c + 1], None, ALU.min).then_inc(wint_ready, 1)
            dve.wait_ge(const_in, 32)
            nc.vector.tensor_copy(t.identb[:], t.ident[:]).then_inc(wint_ready, 1)
            for kc in range(KC):
                dve.wait_ge(wT_ps, kc + 1)
                nc.vector.tensor_copy(wT[:, kc].rearrange("k c m -> k (c m)"), psW[0:KP, kc, 0:WCH * P]).then_inc(wT_ready, 1)
                nc.vector.tensor_copy(t.wpT[:, kc, :], psW[0:KP, kc, WCH * P:WCH * P + D]).then_inc(wT_ready, 1)
            dve.wait_ge(pos_in, 16)
            for g in range(NG):
                lo, hi = g * GT, g * GT + GT
                p0 = lo % TB
                dve.wait_ge(gathered[g], 16 * 2 * GT)
                step(nc.vector.tensor_tensor(seg_rows[:, lo:hi, :], seg_rows[:, lo:hi, :], pos[:, p0:p0 + GT, :], ALU.add))
                step(nc.vector.tensor_tensor(t.h[:, lo:hi, :], seg_rows[:, lo:hi, :], tok_rows[:, lo:hi, :], ALU.add))
                layer_norm_dve(nc, dve, L, t.h, xn, g, GT)
            for g in range(NG):
                dve.wait_ge(y_ready, WCH * (g + 1))
                part = y[:, :, g * GTOK:g * GTOK + GTOK]
                nc.vector.tensor_reduce(yext[:, 0, g, :], part, AX, ALU.max).then_inc(y_ext, 1)
                nc.vector.tensor_reduce(yext[:, 1, g, :], part, AX, ALU.min, negate=True).then_inc(y_ext, 1)
            dve.wait_ge(y_ext, 2 * NG)
            for i in range(2):
                nc.vector.tensor_reduce(ymm[:, i:i + 1], yext[:, i].rearrange("p g c -> p (g c)"), AX, ALU.max).then_inc(ymm_ready, 1)
            dve.wait_ge(ymm_all, 1)
            quant_params_dve(nc, step, t.yall[:], t.ypar[:])
            inv, high = t.ypar[:, 1:2], t.ypar[:, 3:4]

            def quantise(dst, c):
                step(nc.vector.tensor_scalar(y[:, c, :], y[:, c, :], inv, ROUND, ALU.mult, ALU.add))
                return nc.vector.tensor_scalar(dst, y[:, c, :], ROUND, high, ALU.subtract, ALU.min)

            for c in range(2):
                quantise(vint[:, c, :], 4 + c).then_inc(vint_ready, 1)
            for c in range(2):
                step(quantise(t.kf[:, c, :], 2 + c))
            qint = y[:, 5, :].bitcast(BF16)
            dve.wait_ge(vint_ready, 2)
            for c in range(2):
                step(quantise(qint[:, c * TOK:c * TOK + TOK], c))
            for h in range(HEADS):
                c = h // HPC
                last = nc.vector.tensor_scalar(t.qm[:, h, :], qint[:, c * TOK:c * TOK + TOK],
                                               t.headmask[:, h:h + 1], None, ALU.mult)
            step(last)

        @block.scalar
        def _(act):
            def to_xT(g):
                for kc in range(KC):
                    act.wait_ge(xT_ps, KC * g + kc + 1)
                    nc.scalar.copy(xT[:, kc, g * GTOK:g * GTOK + GTOK], psT[0:KP, kc, :]).then_inc(xT_ready, 1)

            def to_y(g):
                for c in range(WCH):
                    n = WCH * g + c
                    act.wait_ge(y_ps, n + 1)
                    nc.scalar.activation(y[:, c, g * GTOK:g * GTOK + GTOK], psY[:, n % 4, :], ACT.Identity,
                                         bias=bias[:, c:c + 1], scale=t.wscale[:, c:c + 1]).then_inc(y_ready, 1)

            act.wait_ge(bias_in, 16 * 6)
            for g in range(NG):
                layer_norm_act(nc, act, L, g, GT)
                to_xT(g)
                to_y(g)
            for b in range(4):
                act.wait_ge(v_ps, b + 1)
                src = psW[:, b % 2, :].rearrange("p (n d) -> p n d", d=2 * P)
                nc.scalar.copy(t.v[:, b * 4:b * 4 + 4, :], src[:, :, 0:D]).then_inc(v_ready, 1)

        @block.tensor
        def _(pe):
            pe.wait_ge(wint_ready, WCH + 3)
            for kc in range(KC):
                for c in range(WCH + 2):
                    mm = nc.tensor.transpose(psW[0:KP, kc, c * P:c * P + P], wint[:, c, kc * KP:kc * KP + KP], t.identb[:])
                mm.then_inc(wT_ps, 1)
            for g in range(NG):
                for kc in range(KC):
                    if g >= 1:
                        pe.wait_ge(xT_ready, KC * (g - 1) + kc + 1)
                    for i in range(GT):
                        pe.wait_ge(L.normed, g * GT + i + 1)
                        mm = nc.tensor.transpose(psT[0:KP, kc, i * P:i * P + P], xn[:, g * GT + i, kc * KP:kc * KP + KP],
                                                 t.ident[:])
                    mm.then_inc(xT_ps, 1)
                pe.wait_ge(xT_ready, KC * (g + 1))
                pe.wait_ge(wT_ready, 2 * KC)
                for c in range(WCH):
                    n = WCH * g + c
                    if n >= 4:
                        pe.wait_ge(y_ready, n - 3)
                    for kc in range(KC):
                        mm = nc.tensor.matmul(psY[:, n % 4, :], wT[:, kc, c, :], xT[:, kc, g * GTOK:g * GTOK + GTOK],
                                              start=(kc == 0), stop=(kc == KC - 1))
                    mm.then_inc(y_ps, 1)
            pe.wait_ge(vint_ready, 2)
            for b in range(4):
                if b >= 2:
                    pe.wait_ge(v_ready, b - 1)
                for i in range(4):
                    tile = b * 4 + i
                    for c in range(2):
                        o = i * 2 * P + c * P
                        mm = nc.tensor.transpose(psW[:, b % 2, o:o + P], vint[:, c, tile * P:tile * P + P], t.identb[:])
                mm.then_inc(v_ps, 1)


def score_extremes(nc, t):
    with ExitStack() as ctx:
        def sem(name):
            return ctx.enter_context(nc.semaphore(name))

        SLOTS = 4
        scores = ctx.enter_context(nc.psum_tensor("x_scores", [P, SLOTS, S], F32))
        rowmin = ctx.enter_context(nc.sbuf_tensor("rowmin", [P, NT * HEADS], F32))
        smm = ctx.enter_context(nc.sbuf_tensor("smm", [P, 2], F32))
        sall = ctx.enter_context(nc.sbuf_tensor("sall", [P, 2], F32))
        spar = ctx.enter_context(nc.sbuf_tensor("spar", [P, 4], F32))
        w = ctx.enter_context(nc.sbuf_tensor("softmax_tmp", [P, 8], F32))
        scores_ready, scores_used = sem("x_scores_ready"), sem("x_scores_used")
        smm_ready, smm_all, dve_step = sem("smm_ready"), sem("smm_all"), sem("x_dve_step")
        block = ctx.enter_context(nc.Block())

        @block.tensor
        def _(pe):
            def row_tile(i, first):
                batch = i // TB
                for h in range(HEADS):
                    if not (first and h < SLOTS):
                        pe.wait_ge(scores_used, i * HEADS + (h + 1 - SLOTS))
                    for j in range(S // 512):
                        mm = nc.tensor.matmul(scores[:, h % SLOTS, j * 512:j * 512 + 512],
                                              t.qm[:, h, bass.ds(i * P, P)],
                                              t.kf[:, h // HPC, bass.ds(batch * S + j * 512, 512)],
                                              start=True, stop=True)
                    mm.then_inc(scores_ready, 1)

            row_tile(0, True)
            with pe.Fori(1, NT) as i:
                row_tile(i, False)

        @block.vector
        def _(dve):
            with dve.Fori(0, NT) as i:
                for h in range(HEADS):
                    dve.wait_ge(scores_ready, i * HEADS + (h + 1))
                    src = scores[:, h % SLOTS, :]
                    nc.vector.tensor_reduce(t.rowmax[:, bass.ds(i * HEADS + h, 1)], src, AX, ALU.max)
                    nc.vector.tensor_reduce(rowmin[:, bass.ds(i * HEADS + h, 1)], src, AX, ALU.min,
                                            negate=True).then_inc(scores_used, 1)
            dve.wait_ge(scores_used, NT * HEADS)
            nc.vector.tensor_reduce(smm[:, 0:1], t.rowmax[:], AX, ALU.max).then_inc(smm_ready, 1)
            nc.vector.tensor_reduce(smm[:, 1:2], rowmin[:], AX, ALU.max).then_inc(smm_ready, 1)
            dve.wait_ge(smm_all, 1)
            step = chain_on(dve, dve_step)
            cl, c2, tmp, flo, cmp = (w[:, i:i + 1] for i in range(5))
            scale_y = t.ypar[:, 0:1]
            step(nc.vector.tensor_scalar(cl, scale_y, scale_y, float(HD) ** -0.5, ALU.mult, ALU.mult))
            step(nc.vector.tensor_scalar(sall[:], sall[:], cl, None, ALU.mult))
            quant_params_dve(nc, step, sall[:], spar[:])
            scale, inv, high = spar[:, 0:1], spar[:, 1:2], spar[:, 3:4]
            step(nc.vector.tensor_tensor(c2, cl, inv, ALU.mult))
            step(nc.vector.tensor_scalar(t.negc2[:], c2, -1.0, None, ALU.mult))
            step(nc.vector.tensor_scalar(t.rowmax[:], t.rowmax[:], c2, ROUND, ALU.mult, ALU.add))
            step(nc.vector.tensor_scalar(t.rowmax[:], t.rowmax[:], ROUND, high, ALU.subtract, ALU.min))

            def floor(dst, src, up):
                step(nc.vector.tensor_scalar(flo, src, ROUND, ROUND, ALU.add, ALU.subtract))
                step(nc.vector.tensor_tensor(cmp, flo, src, ALU.is_lt if up else ALU.is_gt))
                step(nc.vector.tensor_tensor(dst, flo, cmp, ALU.add if up else ALU.subtract))

            X, invX, qoff, Xmax, nhb, K = (t.smpar[:, i:i + 1] for i in range(6))
            b = w[:, 5:6]
            step(nc.vector.tensor_scalar(tmp, inv, X0, None, ALU.mult))
            floor(X, tmp, True)
            step(nc.vector.reciprocal(invX, X))
            step(nc.vector.tensor_scalar(qoff, invX, 0.5, -0.5, ALU.mult, ALU.add))
            step(nc.vector.tensor_scalar(Xmax, X, N_HALVINGS, None, ALU.mult))
            step(nc.vector.tensor_scalar(tmp, inv, B_NUM, None, ALU.mult))
            floor(b, tmp, False)
            step(nc.vector.tensor_scalar(nhb, b, -0.5, None, ALU.mult))
            step(nc.vector.tensor_scalar(tmp, scale, scale, None, ALU.mult))
            step(nc.vector.reciprocal(tmp, tmp))
            step(nc.vector.tensor_scalar(tmp, tmp, C_NUM, None, ALU.mult))
            floor(K, tmp, False)
            step(nc.vector.tensor_tensor(b, b, b, ALU.mult))
            step(nc.vector.scalar_tensor_tensor(out=K, in0=b, scalar=-0.25, in1=K, op0=ALU.mult, op1=ALU.add))

        @block.gpsimd
        def _(pool):
            pool.wait_ge(smm_ready, 2)
            nc.gpsimd.partition_all_reduce(sall[:], smm[:], P, RMAX).then_inc(smm_all, 1)


PAIRS = HEADS // 2
LAST = NT * PAIRS
S_SLOTS = 3


def attention(nc, t):
    with ExitStack() as ctx:
        def sb(name, shape, dt):
            return ctx.enter_context(nc.sbuf_tensor(name, shape, dt))

        def sem(name):
            return ctx.enter_context(nc.semaphore(name))

        scores = ctx.enter_context(nc.psum_tensor("scores", [P, S_SLOTS, S], F32))
        po = ctx.enter_context(nc.psum_tensor("po", [P, 512], F32))
        below = sb("below", [P, 2, 2, S], I16)
        clamped = sb("clamped", [P, 2, S], I16)
        halvings = sb("halvings", [P, 2, S], I16)
        whole = sb("whole", [P, 2, S], I16)
        rest = sb("rest", [P, 2, 2, S], I16)
        half_pow = sb("half_pow", [P, 2, 2, S], I16)
        square = sb("square", [P, 2, 2, S], F32)
        expo = sb("expo", [P, 2, 2, S], F32)
        esum = sb("esum", [P, 2, 2], F32)
        rsum = sb("rsum", [P, 2, 2], F32)
        logp = sb("logp", [P, 2, S], F32)
        ratio = sb("ratio", [P, 2, 2, S], U16)
        power = sb("power", [P, 2, S], BF16)
        field = sb("field", [P, 2, S], U16)
        probs = sb("probs", [P, 2, 2, S], I16)
        probsT = sb("probsT", [P, 2, 2 * TB, P], BF16)
        scores_ready, below_ready, clamped_ready, whole_ready, rest_ready = (
            sem(n) for n in ("scores_ready", "below_ready", "clamped_ready", "whole_ready", "rest_ready"))
        halv_ready, pow_ready, square_ready, expo_ready, rsum_ready, logp_ready, ratio_ready = (
            sem(n) for n in ("halv_ready", "pow_ready", "square_ready", "expo_ready", "rsum_ready", "logp_ready", "ratio_ready"))
        power_ready, field_ready, probs_ready, pv_ready, out_ready = (
            sem(n) for n in ("power_ready", "field_ready", "probs_ready", "pv_ready", "out_ready"))
        turn_starts, below_starts = sem("turn_starts"), sem("below_starts")
        turned = [sem(f"turned{s}") for s in range(2)]
        block = ctx.enter_context(nc.Block())
        X, invX, qoff, Xmax, nhb, K = (t.smpar[:, i:i + 1] for i in range(6))

        def pair_at(i, g, lag):
            row, p = (i, g - lag) if g >= lag else (i - 1, g - lag + PAIRS)
            if type(i) is int and not 0 <= row < NT:
                return None
            return row, p

        def steps(eng, body):
            for g in range(PAIRS):
                body(0, g)
            with eng.Fori(1, NT) as i:
                for g in range(PAIRS):
                    body(i, g)
            for g in range(PAIRS):
                body(NT, g)

        def after(row, p, n):
            return row * PAIRS + (p + 1 + n)

        def exists(row, p, n):
            return type(row) is not int or row * PAIRS + p >= n

        @block.tensor
        def _(pe):
            def make_scores(row, p):
                for h in (2 * p, 2 * p + 1):
                    if exists(row, p, 2) or h >= S_SLOTS:
                        pe.wait_ge(below_ready, row * HEADS + (h + 1 - S_SLOTS))
                    for j in range(S // 512):
                        mm = nc.tensor.matmul(scores[:, h % S_SLOTS, j * 512:j * 512 + 512],
                                              t.qm[:, h, bass.ds(row * P, P)],
                                              t.kf[:, h // HPC, bass.ds((row // TB) * S + j * 512, 512)],
                                              start=True, stop=True)
                    mm.then_inc(scores_ready, 1)

            def times_v(row, p):
                pe.wait_ge(turned[p % 2], (row * (PAIRS // 2) + (p // 2 + 1)) * 16)
                if p == 0 and exists(row, p, PAIRS):
                    pe.wait_ge(out_ready, row)
                for h in (2 * p, 2 * p + 1):
                    for m in range(TB):
                        mm = nc.tensor.matmul(po[:, h * HD:h * HD + HD], probsT[:, p % 2, (h % 2) * TB + m, :],
                                              t.v[:, bass.ds((row // TB) * TB + m, 1), h * HD:h * HD + HD],
                                              start=(m == 0), stop=(m == TB - 1))
                mm.then_inc(pv_ready, 1)

            def body(i, g):
                if at := pair_at(i, g, 0):
                    make_scores(*at)
                if at := pair_at(i, g, 5):
                    times_v(*at)

            steps(pe, body)

        @block.scalar
        def _(act):
            nc.scalar.preload_act_table_set("natural_log_exp_and_others")

            def make_below(row, p):
                if exists(row, p, 2):
                    act.wait_ge(clamped_ready, after(row, p, -2))
                for h in (2 * p, 2 * p + 1):
                    act.wait_ge(scores_ready, row * HEADS + (h + 1))
                    act.sem_inc(below_starts, 1)
                    nc.scalar.activation(below[:, p % 2, h % 2, :], scores[:, h % S_SLOTS, :], ACT.Relu,
                                         bias=t.rowmax[:, bass.ds(row * HEADS + h, 1)], scale=t.negc2[:]).then_inc(below_ready, 1)

            def make_ratio(row, p):
                act.wait_ge(rsum_ready, after(row, p, 0))
                if exists(row, p, 1):
                    act.wait_ge(ratio_ready, after(row, p, -1))
                if exists(row, p, 2):
                    act.wait_ge(power_ready, after(row, p, -2))
                for h in range(2):
                    nc.scalar.activation(logp[:, h, :], expo[:, p % 2, h, :], ACT.Ln,
                                         scale=rsum[:, p % 2, h:h + 1]).then_inc(logp_ready, 1)
                act.wait_ge(logp_ready, after(row, p, 0) * 2)
                nc.scalar.activation(ratio[:, p % 2], logp[:], ACT.Exp, scale=-1.0).then_inc(ratio_ready, 1)

            def make_square(row, p):
                act.wait_ge(rest_ready, after(row, p, 0))
                if exists(row, p, 2):
                    act.wait_ge(expo_ready, after(row, p, -2) * 2)
                nc.scalar.activation(square[:, p % 2], rest[:, p % 2], ACT.Square, bias=nhb).then_inc(square_ready, 1)

            def body(i, g):
                if at := pair_at(i, g, 0):
                    make_below(*at)
                if at := pair_at(i, g, 3):
                    make_ratio(*at)
                if at := pair_at(i, g, 1):
                    make_square(*at)

            steps(act, body)

        @block.vector
        def _(dve):
            def split(row, p):
                dve.wait_ge(below_ready, row * HEADS + (2 * p + 2))
                if exists(row, p, 1):
                    dve.wait_ge(rest_ready, after(row, p, -1))
                nc.vector.tensor_scalar(clamped[:], below[:, p % 2], Xmax, None, ALU.min).then_inc(clamped_ready, 1)
                dve.wait_ge(clamped_ready, after(row, p, 0))
                if exists(row, p, 1):
                    dve.wait_ge(pow_ready, after(row, p, -1))
                nc.vector.tensor_scalar(halvings[:], clamped[:], invX, qoff, ALU.mult, ALU.add).then_inc(halv_ready, 1)
                dve.wait_ge(halv_ready, after(row, p, 0))
                nc.vector.tensor_scalar(whole[:], halvings[:], X, None, ALU.mult).then_inc(whole_ready, 1)
                if exists(row, p, 2):
                    dve.wait_ge(expo_ready, after(row, p, -2) * 2)
                nc.vector.tensor_scalar(half_pow[:, p % 2], halvings[:], -128.0, 127.0 * 128.0,
                                        ALU.mult, ALU.add).then_inc(pow_ready, 1)
                dve.wait_ge(whole_ready, after(row, p, 0))
                if exists(row, p, 2):
                    dve.wait_ge(square_ready, after(row, p, -2))
                nc.vector.tensor_tensor(rest[:, p % 2], clamped[:], whole[:], ALU.subtract).then_inc(rest_ready, 1)

            def exponential(row, p):
                dve.wait_ge(square_ready, after(row, p, 0))
                dve.wait_ge(pow_ready, after(row, p, 0))
                if exists(row, p, 2):
                    dve.wait_ge(logp_ready, after(row, p, -2) * 2)
                for h in range(2):
                    nc.vector.scalar_tensor_tensor(
                        out=expo[:, p % 2, h, :], in0=square[:, p % 2, h, :], scalar=K,
                        in1=half_pow[:, p % 2, h, :].bitcast(BF16), op0=ALU.add, op1=ALU.mult,
                        accum_out=esum[:, p % 2, h:h + 1]).then_inc(expo_ready, 1)
                dve.wait_ge(expo_ready, after(row, p, 0) * 2)
                nc.vector.reciprocal(rsum[:, p % 2, :], esum[:, p % 2, :]).then_inc(rsum_ready, 1)

            def power_of_two(row, p):
                dve.wait_ge(ratio_ready, after(row, p, 0))
                if exists(row, p, 1):
                    dve.wait_ge(field_ready, after(row, p, -1))
                nc.vector.tensor_scalar(power[:], ratio[:, p % 2], POW2, None, ALU.mult).then_inc(power_ready, 1)
                dve.wait_ge(power_ready, after(row, p, 0))
                if exists(row, p, 1):
                    dve.wait_ge(probs_ready, after(row, p, -1))
                nc.vector.tensor_scalar(field[:], power[:].bitcast(U16), EXP_MASK, EXP_MASK,
                                        ALU.bitwise_and, ALU.bitwise_xor).then_inc(field_ready, 1)
                dve.wait_ge(field_ready, after(row, p, 0))
                if exists(row, p, 2):
                    dve.wait_ge(pv_ready, after(row, p, -2))
                nc.vector.tensor_scalar(probs[:, p % 2], field[:], -128.0 * (PSHIFT + 1), 0.0,
                                        ALU.add, ALU.max).then_inc(probs_ready, 1)

            def copy_out(row):
                dve.wait_ge(pv_ready, row * PAIRS + PAIRS)
                nc.vector.tensor_scalar(t.o[:, bass.ds(row, 1), :], po[:, 0:D].unsqueeze(1), 2.0 ** PSHIFT, t.ypar[:, 0:1],
                                        ALU.mult, ALU.mult).then_inc(out_ready, 1)

            def body(i, g):
                if g == PAIRS - 1 and (at := pair_at(i, g, PAIRS)):
                    copy_out(at[0])
                if at := pair_at(i, g, 4):
                    power_of_two(*at)
                if at := pair_at(i, g, 1):
                    split(*at)
                if at := pair_at(i, g, 2):
                    exponential(*at)

            steps(dve, body)

        @block.sync
        def _(sp):
            def turn(row, p):
                sp.wait_ge(probs_ready, after(row, p, 0))
                sp.sem_inc(turn_starts, 1)
                sp.dma_start_transpose(probsT[:, p % 2], probs[:, p % 2].rearrange("p h m -> p (h m)").bitcast(BF16)
                                       ).then_inc(turned[p % 2], 16)

            def body(i, g):
                if at := pair_at(i, g, 4):
                    turn(*at)

            steps(sp, body)


def project_and_route(nc, t, io):
    with ExitStack() as ctx:
        def sb(name, shape, dt):
            return ctx.enter_context(nc.sbuf_tensor(name, shape, dt))

        def sem(name):
            return ctx.enter_context(nc.semaphore(name))

        oext, oall, opar = sb("oext", [P, 2], F32), sb("oall", [P, 2], F32), sb("opar", [P, 4], F32)
        oint = sb("oint", [P, NT, D], BF16)
        oT = sb("oT", [KP, KC, TOK], BF16)
        ones = sb("ones", [P, P], F32)
        diag = sb("diag", [P, 2, P], F32)
        srow = sb("srow", [P, D], F32)
        brow = sb("brow", [P, D], F32)
        p = sb("p_out", [P, NT, D], F32)
        pext, pall, ppar = sb("pext", [P, 2], F32), sb("pall", [P, 2], F32), sb("ppar", [P, 4], F32)
        gT = sb("gT", [KP, KC, E], F32)
        rank = sb("rank_sb", [P, E], F32)
        prob = sb("prob", [P, NT, E], F32)
        left = sb("left", [P, NT, E], F32)
        pick = sb("pick", [P, 2, NT, E], F32)
        top = sb("top", [P, 3, NT], F32)
        psT = ctx.enter_context(nc.psum_tensor("r_psT", [P, 2, 512], F32))
        psO = ctx.enter_context(nc.psum_tensor("psO", [P, 2, 1024], BF16))
        psP = ctx.enter_context(nc.psum_tensor("psP", [P, 2, 512], F32))
        psR = ctx.enter_context(nc.psum_tensor("psR", [P, 512], F32))
        psG = ctx.enter_context(nc.psum_tensor("psG", [P, 512], F32))
        xn = p
        L = Norm(sb, sem, "norm2")
        rows_in, gate_in, dve_step, oext_ready, oall_ready, oint_ready, ones_ready, diag_ready, srow_ps = (
            sem(n) for n in ("rows_in", "gate_in", "r_dve_step", "oext_ready", "oall_ready", "oint_ready", "ones_ready",
                             "diag_ready", "srow_ps"))
        oT_ps, oT_ready, p_ps, p_used, pext_ready, pall_ready, xT_ps, xT_ready, gate_ps, diff_ready, exp_ready = (
            sem(n) for n in ("oT_ps", "oT_ready", "p_ps", "p_used", "pext_ready", "pall_ready", "r_xT_ps", "r_xT_ready",
                             "gate_ps", "diff_ready", "exp_ready"))
        block = ctx.enter_context(nc.Block())

        @block.sync
        def _(sp):
            sp.dma_start(brow[:], io.b_proj.partition_broadcast(P)).then_inc(rows_in, 16)
            sp.dma_start(rank[:], io.rank).then_inc(rows_in, 16)
            with nc.allow_non_contiguous_dma("gate weights, transposed"):
                for kc in range(KC):
                    sp.dma_start(gT[:, kc, :], io.gate_w[:, kc * KP:kc * KP + KP].rearrange("e k -> k e")).then_inc(gate_in, 16)

        @block.gpsimd
        def _(pool):
            nc.gpsimd.memset(ones[:], 1.0).then_inc(ones_ready, 1)
            pool.wait_ge(oext_ready, 2)
            nc.gpsimd.partition_all_reduce(oall[:], oext[:], P, RMAX).then_inc(oall_ready, 1)
            pool.wait_ge(pext_ready, 2)
            nc.gpsimd.partition_all_reduce(pall[:], pext[:], P, RMAX).then_inc(pall_ready, 1)

        @block.vector
        def _(dve):
            step = L.chain = chain_on(dve, dve_step)
            flat_o, flat_p = t.o[:].rearrange("p r d -> p (r d)"), p[:].rearrange("p r d -> p (r d)")
            for c in range(2):
                nc.vector.tensor_scalar(diag[:, c, :], t.ident[:], t.wscale[:, WCH + c:WCH + c + 1], None,
                                        ALU.mult).then_inc(diag_ready, 1)
            nc.vector.tensor_reduce(oext[:, 0:1], flat_o, AX, ALU.max).then_inc(oext_ready, 1)
            nc.vector.tensor_reduce(oext[:, 1:2], flat_o, AX, ALU.min, negate=True).then_inc(oext_ready, 1)
            dve.wait_ge(oall_ready, 1)
            quant_params_dve(nc, step, oall[:], opar[:])
            for g in range(NG):
                part = t.o[:, g * GT:g * GT + GT, :]
                step(nc.vector.tensor_scalar(part, part, opar[:, 1:2], ROUND, ALU.mult, ALU.add))
                nc.vector.tensor_scalar(oint[:, g * GT:g * GT + GT, :], part, ROUND, opar[:, 3:4],
                                        ALU.subtract, ALU.min).then_inc(oint_ready, 1)
            dve.wait_ge(srow_ps, 1)
            step(nc.vector.tensor_copy(srow[:], psR[:, 0:D]))
            dve.wait_ge(rows_in, 32)
            for b in range(NT // 2):
                dve.wait_ge(p_ps, b + 1)
                dst = p[:, 2 * b:2 * b + 2, :]
                src = psP[:, b % 2, 0:2 * D].rearrange("p (r d) -> p r d", r=2)
                nc.vector.scalar_tensor_tensor(out=dst, in0=src, scalar=opar[:, 0:1],
                                               in1=srow[:].unsqueeze(1).broadcast_to([P, 2, D]),
                                               op0=ALU.mult, op1=ALU.mult).then_inc(p_used, 1)
                dve.wait_ge(p_used, b + 1)
                step(nc.vector.tensor_tensor(dst, dst, brow[:].unsqueeze(1).broadcast_to([P, 2, D]), ALU.add))
            nc.vector.tensor_reduce(pext[:, 0:1], flat_p, AX, ALU.max).then_inc(pext_ready, 1)
            nc.vector.tensor_reduce(pext[:, 1:2], flat_p, AX, ALU.min, negate=True).then_inc(pext_ready, 1)
            dve.wait_ge(pall_ready, 1)
            quant_params_dve(nc, step, pall[:], ppar[:])
            for g in range(NG):
                lo, hi = g * GT, g * GT + GT
                part = p[:, lo:hi, :]
                step(nc.vector.tensor_scalar(part, part, ppar[:, 1:2], ROUND, ALU.mult, ALU.add))
                step(nc.vector.tensor_scalar(part, part, ROUND, ppar[:, 3:4], ALU.subtract, ALU.min))
                step(nc.vector.scalar_tensor_tensor(out=t.h[:, lo:hi, :], in0=part, scalar=ppar[:, 0:1],
                                                    in1=t.h[:, lo:hi, :], op0=ALU.mult, op1=ALU.add))
                layer_norm_dve(nc, dve, L, t.h, xn, g, GT)
            def per_token(a):
                return a.unsqueeze(2).broadcast_to([P, NT, E])

            ranks = rank[:].unsqueeze(1).broadcast_to([P, NT, E])
            logits = psG[:, 0:NT * E].rearrange("p (r e) -> p r e", e=E)
            dve.wait_ge(gate_ps, NT)
            step(nc.vector.tensor_reduce(top[:, 0, :], logits, AX, ALU.max))
            nc.vector.tensor_tensor(left[:], logits, per_token(top[:, 0, :]), ALU.subtract).then_inc(diff_ready, 1)
            dve.wait_ge(exp_ready, 1)
            step(nc.vector.tensor_reduce(top[:, 0, :], prob[:], AX, ALU.add))
            step(nc.vector.reciprocal(top[:, 1, :], top[:, 0, :]))
            step(nc.vector.tensor_tensor(prob[:], prob[:], per_token(top[:, 1, :]), ALU.mult))
            step(nc.vector.tensor_copy(left[:], prob[:]))
            for n in range(2):
                one = pick[:, n]
                step(nc.vector.tensor_reduce(top[:, n, :], left[:], AX, ALU.max))
                step(nc.vector.tensor_tensor(one, left[:], per_token(top[:, n, :]), ALU.is_equal))
                step(nc.vector.tensor_tensor(one, one, ranks, ALU.mult))
                step(nc.vector.tensor_reduce(top[:, 2, :], one, AX, ALU.max))
                step(nc.vector.tensor_tensor(one, one, per_token(top[:, 2, :]), ALU.is_equal))
                step(nc.vector.scalar_tensor_tensor(out=left[:], in0=one, scalar=-2.0, in1=left[:],
                                                    op0=ALU.mult, op1=ALU.add))
            step(nc.vector.tensor_tensor(top[:, 2, :], top[:, 0, :], top[:, 1, :], ALU.add))
            step(nc.vector.tensor_scalar(top[:, 2, :], top[:, 2, :], 1e-09, None, ALU.add))
            step(nc.vector.reciprocal(top[:, 2, :], top[:, 2, :]))
            step(nc.vector.tensor_tensor(prob[:], prob[:], per_token(top[:, 2, :]), ALU.mult))
            step(nc.vector.tensor_tensor(pick[:, 0], pick[:, 0], pick[:, 1], ALU.add))
            step(nc.vector.tensor_tensor(t.share[:].rearrange("p e r -> p r e"), prob[:], pick[:, 0], ALU.mult))

        @block.scalar
        def _(act):
            for g in range(NG):
                for kc in range(KC):
                    act.wait_ge(oT_ps, KC * g + kc + 1)
                    nc.scalar.copy(oT[:, kc, g * GTOK:g * GTOK + GTOK], psO[0:KP, kc, 0:GTOK]).then_inc(oT_ready, 1)
            for g in range(NG):
                layer_norm_act(nc, act, L, g, GT)
                for kc in range(KC):
                    act.wait_ge(xT_ps, KC * g + kc + 1)
                    nc.scalar.copy(t.x2T[:, kc, g * GTOK:g * GTOK + GTOK], psT[0:KP, kc, :]).then_inc(xT_ready, 1)
            act.wait_ge(diff_ready, 1)
            nc.scalar.activation(prob[:], left[:], ACT.Exp).then_inc(exp_ready, 1)

        @block.tensor
        def _(pe):
            pe.wait_ge(ones_ready, 1)
            pe.wait_ge(diag_ready, 2)
            nc.tensor.matmul(psR[:, 0:P], ones[:], diag[:, 0, :], start=True, stop=True)
            nc.tensor.matmul(psR[:, P:D], ones[:], diag[:, 1, 0:D - P], start=True, stop=True).then_inc(srow_ps, 1)
            for g in range(NG):
                pe.wait_ge(oint_ready, g + 1)
                for kc in range(KC):
                    if g >= 1:
                        pe.wait_ge(oT_ready, KC * (g - 1) + kc + 1)
                    for i in range(GT):
                        mm = nc.tensor.transpose(psO[0:KP, kc, i * P:i * P + P],
                                                 oint[:, g * GT + i, kc * KP:kc * KP + KP], t.identb[:])
                    mm.then_inc(oT_ps, 1)
                pe.wait_ge(oT_ready, KC * (g + 1))
                for b in (2 * g, 2 * g + 1):
                    if b >= 2:
                        pe.wait_ge(p_used, b - 1)
                    for i in range(2):
                        tile = 2 * b + i
                        for kc in range(KC):
                            mm = nc.tensor.matmul(psP[:, b % 2, i * D:i * D + D], oT[:, kc, tile * P:tile * P + P],
                                                  t.wpT[:, kc, :], start=(kc == 0), stop=(kc == KC - 1))
                    mm.then_inc(p_ps, 1)
            pe.wait_ge(gate_in, 16 * KC)
            for g in range(NG):
                for kc in range(KC):
                    if g >= 1:
                        pe.wait_ge(xT_ready, KC * (g - 1) + kc + 1)
                    for i in range(GT):
                        pe.wait_ge(L.normed, g * GT + i + 1)
                        mm = nc.tensor.transpose(psT[0:KP, kc, i * P:i * P + P], xn[:, g * GT + i, kc * KP:kc * KP + KP],
                                                 t.ident[:])
                    mm.then_inc(xT_ps, 1)
                pe.wait_ge(xT_ready, KC * (g + 1))
                for i in range(GT):
                    tile = g * GT + i
                    for kc in range(KC):
                        mm = nc.tensor.matmul(psG[:, tile * E:tile * E + E], t.x2T[:, kc, tile * P:tile * P + P],
                                              gT[:, kc, :], start=(kc == 0), stop=(kc == KC - 1))
                    mm.then_inc(gate_ps, 1)


def experts(nc, t, io):
    with ExitStack() as ctx:
        def sb(name, shape, dt):
            return ctx.enter_context(nc.sbuf_tensor(name, shape, dt))

        def sem(name):
            return ctx.enter_context(nc.semaphore(name))

        STEPS = 2 * NG
        HSLOTS = 4
        w1s = sb("w1s", [KP, 2, KC, H], F32)
        w2s = sb("w2s", [P, 2, HC, D], F32)
        b1c = sb("b1c", [P, E * HC], F32)
        b2r = sb("b2r", [P, E, D], F32)
        hid = sb("hid", [P, 2, HC, GTOK], F32)
        part = sb("part", [P, GT, D], F32)
        psH = ctx.enter_context(nc.psum_tensor("psH", [P, HSLOTS, 512], F32))
        psE = ctx.enter_context(nc.psum_tensor("psE", [P, GT, 512], F32))
        hid_ps, hid_ready, out_ps, part_ready, added = (sem(n) for n in ("hid_ps", "hid_ready", "out_ps", "part_ready", "added"))
        bias_in, stored, gelu_starts = sem("f_bias_in"), sem("stored"), sem("gelu_starts")
        weights_in = [sem(f"weights_in{s}") for s in range(2)]
        block = ctx.enter_context(nc.Block())

        def steps(eng, body, lag):
            for s in range(STEPS):
                body(0, s)
            with eng.Fori(1, E // 2) as i:
                for s in range(STEPS):
                    body(i, s)
            if lag:
                body(E // 2, 0)

        def step_at(i, s, lag):
            row, q = (i, s - lag) if s >= lag else (i - 1, s - lag + STEPS)
            if type(i) is int and not 0 <= row < E // 2:
                return None
            return row, q

        @block.sync
        def _(sp):
            with nc.allow_non_contiguous_dma("one bias per partition"):
                sp.dma_start(b1c[:], io.b1.rearrange("e (j p) -> p (e j)", p=P)).then_inc(bias_in, 16)
            sp.dma_start(b2r[:].rearrange("p e d -> p (e d)"), io.b2.rearrange("e d -> (e d)").partition_broadcast(P)).then_inc(bias_in, 16)

            def load(i, s):
                if type(i) is not int or i > 0:
                    sp.wait_ge(out_ps, i * STEPS + (s + 1) * NG - STEPS)
                e = i * 2 + s
                sp.dma_start(w1s[:, s], io.w1[bass.ds(e, 1)].rearrange("e (c k) h -> k (e c) h", k=KP)).then_inc(weights_in[s], 16)
                sp.dma_start(w2s[:, s], io.w2[bass.ds(e, 1)].rearrange("e (j k) d -> k (e j) d", k=P)).then_inc(weights_in[s], 16)

            for s in range(2):
                load(0, s)
            with sp.Fori(1, E // 2) as i:
                for s in range(2):
                    load(i, s)
            for g in range(NG):
                sp.wait_ge(added, E * NT - NT + (g + 1) * GT)
                for r in range(g * GT, g * GT + GT):
                    b, c = divmod(r, TB)
                    sp.dma_start(io.out[b, c * P:c * P + P, :], t.h[:, r, :]).then_inc(stored, 16)
            sp.wait_ge(stored, 16 * NT)

        @block.tensor
        def _(pe):
            def hidden(i, s):
                if s % NG == 0:
                    pe.wait_ge(weights_in[s // NG], i * 32 + 32)
                for j in range(HC):
                    n = s * HC + j
                    if n >= HSLOTS or type(i) is not int:
                        pe.wait_ge(hid_ready, i * (STEPS * HC) + (n + 1 - HSLOTS))
                    g = s % NG
                    for kc in range(KC):
                        mm = nc.tensor.matmul(psH[:, n % HSLOTS, :], w1s[:, s // NG, kc, j * P:j * P + P],
                                              t.x2T[:, kc, g * GTOK:g * GTOK + GTOK], start=(kc == 0), stop=(kc == KC - 1))
                    mm.then_inc(hid_ps, 1)

            def output(i, s):
                pe.wait_ge(hid_ready, i * (STEPS * HC) + (s + 1) * HC)
                for r in range(GT):
                    if s >= 1 or type(i) is not int or i > 0:
                        pe.wait_ge(part_ready, i * (STEPS * GT) + (s * GT + r + 1 - GT))
                    for j in range(HC):
                        mm = nc.tensor.matmul(psE[:, r, 0:D], hid[:, s % 2, j, r * P:r * P + P], w2s[:, s // NG, j, :],
                                              start=(j == 0), stop=(j == HC - 1))
                mm.then_inc(out_ps, 1)

            def body(i, s):
                if type(i) is not int or i < E // 2:
                    hidden(i, s)
                if at := step_at(i, s, 1):
                    output(*at)

            steps(pe, body, 1)

        @block.scalar
        def _(act):
            act.wait_ge(bias_in, 32)

            def body(i, s):
                if type(i) is not int or i > 0 or s >= 2:
                    act.wait_ge(out_ps, i * STEPS + (s - 1))
                for j in range(HC):
                    n = s * HC + j
                    act.wait_ge(hid_ps, i * (STEPS * HC) + (n + 1))
                    act.sem_inc(gelu_starts, 1)
                    nc.scalar.activation(hid[:, s % 2, j, :], psH[:, n % HSLOTS, :], ACT.Gelu,
                                         bias=b1c[:, bass.ds((i * 2 + s // NG) * HC + j, 1)]).then_inc(hid_ready, 1)

            steps(act, body, 0)

        @block.vector
        def _(dve):
            dve.wait_ge(bias_in, 32)

            def body(i, s):
                e = i * 2 + s // NG
                g = s % NG
                dve.wait_ge(out_ps, i * STEPS + (s + 1))
                for r in range(GT):
                    if s >= 1 or type(i) is not int or i > 0:
                        dve.wait_ge(added, i * (STEPS * GT) + (s * GT + r + 1 - GT))
                    nc.vector.tensor_tensor(part[:, r, :].unsqueeze(1), psE[:, r, 0:D].unsqueeze(1), b2r[:, bass.ds(e, 1), :],
                                            ALU.add).then_inc(part_ready, 1)
                for r in range(GT):
                    dve.wait_ge(part_ready, i * (STEPS * GT) + (s * GT + r + 1))
                    tile = g * GT + r
                    nc.vector.scalar_tensor_tensor(out=t.h[:, tile, :], in0=part[:, r, :],
                                                   scalar=t.share[:].rearrange("p e r -> p (e r)")[:, bass.ds(e * NT + tile, 1)],
                                                   in1=t.h[:, tile, :], op0=ALU.mult, op1=ALU.add).then_inc(added, 1)

            steps(dve, body, 0)


def program(nc, x, mask, token_table, segm_table, w_qkv, b_qkv, w_proj, b_proj, gate_w, w1, b1, w2, b2,
            pos, ident, headmask, rank, out, dump=None):
    io = Inputs()
    io.x, io.mask, io.token_table, io.segm_table = x, mask, token_table, segm_table
    io.w_qkv, io.b_qkv, io.w_proj, io.b_proj, io.gate_w = w_qkv, b_qkv, w_proj, b_proj, gate_w
    io.w1, io.b1, io.w2, io.b2, io.out = w1, b1, w2, b2, out
    io.pos, io.ident, io.headmask, io.rank = pos, ident, headmask, rank
    with ExitStack() as ctx:
        def sb(name, shape, dt):
            return ctx.enter_context(nc.sbuf_tensor(name, shape, dt))

        t = Shared()
        t.h = sb("h", [P, NT, D], F32)
        t.v = sb("v", [P, NT, D], BF16)
        t.o = sb("o", [P, NT, D], F32)
        t.ident = sb("ident_sb", [P, P], F32)
        t.identb = sb("identb", [P, P], BF16)
        t.headmask = sb("headmask_sb", [P, HEADS], F32)
        t.wscale = sb("wscale", [P, WCH + 2], F32)
        t.wpT = sb("wpT", [KP, KC, D], BF16)
        t.yall, t.ypar = sb("yall", [P, 2], F32), sb("ypar", [P, 4], F32)
        t.rowmax = sb("rowmax", [P, NT * HEADS], F32)
        t.negc2, t.smpar = sb("negc2", [P, 1], F32), sb("smpar", [P, 6], F32)
        with ExitStack() as qk:
            t.kf = qk.enter_context(nc.sbuf_tensor("kf", [P, 2, TOK], BF16))
            t.qm = qk.enter_context(nc.sbuf_tensor("qm", [P, HEADS, TOK], BF16))
            load_weights_and_tokens(nc, t, io)
            if dump == "A":
                return dump_all(nc, t, out)
            score_extremes(nc, t)
            if dump == "B":
                return dump_all(nc, t, out)
            attention(nc, t)
            if dump == "C":
                return dump_all(nc, t, out)
        t.x2T, t.share = sb("x2T", [KP, KC, TOK], F32), sb("share", [P, E, NT], F32)
        project_and_route(nc, t, io)
        if dump == "D":
            return dump_all(nc, t, out)
        experts(nc, t, io)


_INS = ['x', 'mask_BS_i2_0', 'L0_tok_token_table', 'L0_tok_segm_table', 'L0_attn_w_qkv', 'L0_attn_b_qkv',
        'L0_attn_w_proj', 'L0_attn_b_proj', 'L0_ffn_gate_w', 'L0_ffn_w1', 'L0_ffn_b1', 'L0_ffn_w2', 'L0_ffn_b2']
_OUTS = [((B, S, D), 'float32')]


def shape_constants():
    import numpy as np
    f = np.float32
    feature = np.arange(D, dtype=f)
    angle = np.arange(S, dtype=f)[:, None] / np.power(f(10000.0), np.floor(feature / f(2)) * f(2) / f(D))[None, :]
    pos = np.where(np.arange(D) % 2 == 0, np.sin(angle), np.cos(angle)).astype(f)
    headmask = (np.arange(P)[:, None] // HD == np.arange(HEADS)[None, :] % HPC).astype(f)
    rank = np.repeat(np.arange(E, 0, -1, dtype=f)[None, :], P, axis=0)
    return {'pos': pos, 'ident': np.eye(P, dtype=f), 'headmask': headmask, 'rank': rank}


def kernel(**inputs):
    import numpy as _np
    import concourse.bacc as _bacc
    from concourse import mybir as _mybir
    from concourse.bass_utils import run_bass_kernel_spmd as _run

    nc = _bacc.Bacc("TRN2", target_bir_lowering=False, num_devices=1)
    arrays, args = {}, []
    for name, a in [(n, inputs[n]) for n in _INS] + list(shape_constants().items()):
        a = _np.ascontiguousarray(a)
        arrays[f"in_{name}_dram"] = a
        args.append(nc.dram_tensor(f"in_{name}_dram", a.shape, _mybir.dt.from_np(a.dtype), kind="ExternalInput").ap())
    for i, (shape, dtype) in enumerate(_OUTS):
        dt = _mybir.dt.from_np(_np.dtype(dtype))
        args.append(nc.dram_tensor(f"out_{i}_dram", shape, dt, kind="ExternalOutput").ap())
    program(nc, *args)
    r = _run(nc, [arrays], core_ids=[0])
    got = tuple(r.results[0][f"out_{i}_dram"] for i in range(len(_OUTS)))
    return got[0]
```

```python
from contextlib import ExitStack

import concourse.bass as bass
from concourse import mybir



ALU = mybir.AluOpType
ACT = mybir.ActivationFunctionType
F32 = mybir.dt.float32
BF16 = mybir.dt.bfloat16
F16 = mybir.dt.float16
I16 = mybir.dt.int16
U16 = mybir.dt.uint16
I32 = mybir.dt.int32
U32 = mybir.dt.uint32
AX = mybir.AxisListType.X
RMAX = bass.bass_isa.ReduceOp.max
RADD = bass.bass_isa.ReduceOp.add

P = 128
B, S = 2, 1024
TOK = B * S
NT = TOK // P
TB = S // P
D = 192
KC = 2
KP = D // KC
HEADS, HD = 12, 16
HPC = P // HD
NG = 4
GT = NT // NG
GTOK = GT * P
WCH = 6
VOCAB, SEGS = 8000, 3
E, H = 8, 768
HC = H // P

XCH, WCHUNKS = 5, 3
WEIGHTS_OF = (0, 1, 2, 0, 1)
HALF = P // 2
X_SCALE = 4096.0
EXP_BITS = 0x7F800000

ROUND = 12582912.0
EPS_SCALE = 1.1920928955078125e-07
LN_EPS = 1e-05
QMAX = 255.0
BIG = 3.0e38

X0 = 0.6931
C0 = 0.35815147
B_NUM = 0.96963238 / C0
C_NUM = 1.0 / C0
N_HALVINGS = 30.0
POW2 = 4.0 / 3.0 * (1.0 - 2.0 ** -9) * (1.0 + 1e-6)
EXP_MASK = 0x7F80
PSHIFT = 111
POW_SHIFT = 2.0 ** 16
POW_LIMIT = 2.0 ** 32
POW_FLIP = 159 << 7


class Norm:

    def __init__(self, sb, sem, name):
        self.stats = sb(name + "_stats", [P, NT, 6], F32)
        self.meanvar = sb(name + "_meanvar", [P, NT, 2], F32)
        self.vareps = sb(name + "_vareps", [P, NT], F32)
        self.root = sb(name + "_root", [P, NT], F32)
        self.tmp = sb(name + "_tmp", [P, NT], F32)
        self.rstd = sb(name + "_rstd", [P, NT], F32)
        self.stats_done = sem(name + "_stats_done")
        self.aggr_done = sem(name + "_aggr_done")
        self.var_ready = sem(name + "_var_ready")
        self.root_ready = sem(name + "_root_ready")
        self.normed = sem(name + "_normed")


def layer_norm_dve(nc, dve, L, src, dst, g, n):
    lo, hi = n * g, n * g + n
    for r in range(lo, hi):
        nc.vector.bn_stats(L.stats[:, r, :], src[:, r, :]).then_inc(L.stats_done, 1)
    for r in range(lo, hi):
        dve.wait_ge(L.stats_done, r + 1)
        nc.vector.bn_aggr(L.meanvar[:, r, :], L.stats[:, r, :]).then_inc(L.aggr_done, 1)
    dve.wait_ge(L.aggr_done, hi)
    var, root = L.vareps[:, lo:hi], L.root[:, lo:hi]
    nc.vector.tensor_scalar(var, L.meanvar[:, lo:hi, 1], LN_EPS, None, ALU.add).then_inc(L.var_ready, 1)
    dve.wait_ge(L.root_ready, g + 1)
    step = L.chain
    step(nc.vector.reciprocal(L.tmp[:, lo:hi], root))
    step(nc.vector.tensor_tensor(L.tmp[:, lo:hi], L.tmp[:, lo:hi], var, ALU.mult))
    step(nc.vector.scalar_tensor_tensor(out=L.tmp[:, lo:hi], in0=L.tmp[:, lo:hi], scalar=0.0, in1=root,
                                        op0=ALU.add, op1=ALU.add))
    step(nc.vector.tensor_scalar(L.tmp[:, lo:hi], L.tmp[:, lo:hi], 0.5, None, ALU.mult))
    step(nc.vector.reciprocal(L.rstd[:, lo:hi], L.tmp[:, lo:hi]))
    for r in range(lo, hi):
        nc.vector.tensor_scalar(dst[:, r, :], src[:, r, :], L.meanvar[:, r, 0:1], L.rstd[:, r:r + 1],
                                ALU.subtract, ALU.mult).then_inc(L.normed, 1)


def layer_norm_act(nc, act, L, g, n):
    act.wait_ge(L.var_ready, g + 1)
    nc.scalar.activation(L.root[:, n * g:n * g + n], L.vareps[:, n * g:n * g + n], ACT.Sqrt).then_inc(L.root_ready, 1)


def chain_on(eng, sem):
    count = [0]

    def step(ins):
        count[0] += 1
        ins.then_inc(sem, 1)
        eng.wait_ge(sem, count[0])

    return step


def quant_params_dve(nc, step, ext, pr):
    scale, inv, low, high = (pr[:, i:i + 1] for i in range(4))
    step(nc.vector.tensor_scalar(ext, ext, 0.0, None, ALU.max))
    step(nc.vector.tensor_tensor(scale, ext[:, 0:1], ext[:, 1:2], ALU.add))
    step(nc.vector.tensor_scalar(scale, scale, 1.0 / QMAX, EPS_SCALE, ALU.mult, ALU.max))
    step(nc.vector.reciprocal(inv, scale))
    step(nc.vector.tensor_scalar(low, ext[:, 1:2], inv, ROUND, ALU.mult, ALU.add))
    step(nc.vector.tensor_scalar(low, low, ROUND, -1.0, ALU.subtract, ALU.mult))
    step(nc.vector.tensor_scalar(high, low, QMAX, None, ALU.add))


class Inputs:
    pass


class Shared:
    pass


def load_weights_and_tokens(nc, t, io):
    with ExitStack() as ctx:
        def sb(name, shape, dt):
            return ctx.enter_context(nc.sbuf_tensor(name, shape, dt))

        def sem(name):
            return ctx.enter_context(nc.semaphore(name))

        ids = sb("ids", [P, 2, NT], I32)
        idf = sb("idf", [P, 2, NT], F32)
        wrap = sb("wrap", [P, 2, NT], F32)
        rows = sb("rows", [P, 2, NT], U32)
        tok_rows = sb("tok_rows", [P, NT, D], F32)
        seg_rows = sb("seg_rows", [P, NT, D], F32)
        pos = sb("pos_sb", [P, TB, D], F32)
        xn = tok_rows
        xT = sb("xT", [KP, KC, TOK], F32)
        wraw = sb("wraw", [P, WCH + 2, D], F32)
        wint = sb("wint", [P, WCH + 2, D], BF16)
        wext = sb("wext", [P, 6, WCH + 2], F32)
        wT = sb("wT", [KP, KC, WCH, P], F32)
        bias = sb("bias", [P, WCH], F32)
        y = sb("y", [P, WCH, TOK], F32)
        yext = sb("yext", [P, 2, NG, WCH], F32)
        ymm = sb("ymm", [P, 2], F32)
        vint = seg_rows[:].rearrange("p r d -> p (r d)")[:, 0:TOK].bitcast(BF16).rearrange(
            "p (c n) -> p c n", c=2)
        psT = ctx.enter_context(nc.psum_tensor("psT", [P, 2, 512], F32))
        psW = ctx.enter_context(nc.psum_tensor("psW", [P, 2, 1024], BF16))
        psY = ctx.enter_context(nc.psum_tensor("psY", [P, 4, 512], F32))

        L = Norm(sb, sem, "norm1")
        ids_in, w_in, pos_in, const_in, bias_in = (sem(n) for n in ("ids_in", "w_in", "pos_in", "const_in", "bias_in"))
        pad_ready, rows_ready, dve_step = sem("pad_ready"), sem("rows_ready"), sem("dve_step")
        gathered = [sem(f"gathered{g}") for g in range(NG)]
        wint_ready, wT_ps, wT_ready = sem("wint_ready"), sem("wT_ps"), sem("wT_ready")
        xT_ps, xT_ready, y_ps, y_ready, y_ext = (sem(n) for n in ("xT_ps", "xT_ready", "y_ps", "y_ready", "y_ext"))
        ymm_ready, ymm_all, vint_ready, v_ps, v_ready = (
            sem(n) for n in ("ymm_ready", "ymm_all", "vint_ready", "v_ps", "v_ready"))
        sum_done, h_ready = sem("sum_done"), sem("h_ready")
        n_w_loads = WCH + 2

        block = ctx.enter_context(nc.Block())

        @block.sync
        def _(sp):
            with nc.allow_non_contiguous_dma("token ids"):
                for i, src in enumerate((io.x, io.mask)):
                    sp.dma_start(ids[:, i, :], src.rearrange("b s -> (b s)").rearrange("(r p) -> p r", p=P)).then_inc(ids_in, 16)
            sp.wait_ge(pad_ready, 1)
            for part in range(4):
                src, r0 = (io.w_qkv, part * D) if part < 3 else (io.w_proj, 0)
                sp.dma_start(wraw[:, 2 * part, :], src[r0:r0 + P, :]).then_inc(w_in, 16)
                sp.dma_start(wraw[0:D - P, 2 * part + 1, :], src[r0 + P:r0 + D, :]).then_inc(w_in, 16)
            sp.dma_start(pos[:], io.pos.rearrange("(r p) d -> p r d", p=P)).then_inc(pos_in, 16)
            sp.dma_start(t.ident[:], io.ident).then_inc(const_in, 16)
            sp.dma_start(t.headmask[:], io.headmask).then_inc(const_in, 16)
            sp.wait_ge(pad_ready, 2)
            with nc.allow_non_contiguous_dma("one bias per partition"):
                for part in range(3):
                    r0 = part * D
                    sp.dma_start(bias[:, 2 * part:2 * part + 1], io.b_qkv[r0:r0 + P].unsqueeze(1)).then_inc(bias_in, 16)
                    sp.dma_start(bias[0:D - P, 2 * part + 1:2 * part + 2],
                                 io.b_qkv[r0 + P:r0 + D].unsqueeze(1)).then_inc(bias_in, 16)

        @block.gpsimd
        def _(pool):
            nc.gpsimd.memset(wraw[:], 0.0).then_inc(pad_ready, 1)
            nc.gpsimd.memset(bias[:], 0.0).then_inc(pad_ready, 1)
            pool.wait_ge(rows_ready, 2)
            for g in range(NG):
                for r in range(g * GT, g * GT + GT):
                    for i, (dst, table) in enumerate(((tok_rows, io.token_table), (seg_rows, io.segm_table))):
                        pool.indirect_dma_start(
                            out=dst[:, r, :], out_offset=None, in_=table,
                            in_offset=bass.IndirectOffsetOnAxis(ap=rows[:, i, r:r + 1], axis=0),
                        ).then_inc(gathered[g], 16)
            pool.wait_ge(ymm_ready, 2)
            nc.gpsimd.partition_all_reduce(t.yall[:], ymm[:], P, RMAX).then_inc(ymm_all, 1)

        @block.vector
        def _(dve):
            step = L.chain = chain_on(dve, dve_step)
            dve.wait_ge(ids_in, 32)
            for i, n in enumerate((VOCAB, SEGS)):
                step(nc.vector.tensor_scalar(wrap[:, i, :], ids[:, i, :], 0.0, float(n), ALU.is_lt, ALU.mult))
                step(nc.vector.tensor_tensor(idf[:, i, :], wrap[:, i, :], ids[:, i, :], ALU.add))
                nc.vector.tensor_scalar(rows[:, i, :], idf[:, i, :], 0.0, float(n - 1), ALU.max, ALU.min).then_inc(rows_ready, 1)
            dve.wait_ge(w_in, 16 * n_w_loads)
            mx, nmn, sc, inv, low, high = (wext[:, i, :] for i in range(6))
            step(nc.vector.tensor_reduce(mx, wraw[:], AX, ALU.max))
            step(nc.vector.tensor_reduce(nmn, wraw[:], AX, ALU.min, negate=True))
            step(nc.vector.tensor_scalar(wext[:, 0:2, :], wext[:, 0:2, :], 0.0, None, ALU.max))
            step(nc.vector.tensor_tensor(sc, mx, nmn, ALU.add))
            step(nc.vector.tensor_scalar(t.wscale[:], sc, 1.0 / QMAX, EPS_SCALE, ALU.mult, ALU.max))
            step(nc.vector.reciprocal(inv, t.wscale[:]))
            step(nc.vector.tensor_tensor(low, nmn, inv, ALU.mult))
            step(nc.vector.tensor_scalar(low, low, ROUND, ROUND, ALU.add, ALU.subtract))
            step(nc.vector.tensor_scalar(low, low, -1.0, None, ALU.mult))
            step(nc.vector.tensor_scalar(high, low, QMAX, None, ALU.add))
            for c in range(WCH + 2):
                step(nc.vector.tensor_scalar(wraw[:, c, :], wraw[:, c, :], inv[:, c:c + 1], ROUND, ALU.mult, ALU.add))
                step(nc.vector.tensor_scalar(wraw[:, c, :], wraw[:, c, :], ROUND, low[:, c:c + 1], ALU.subtract, ALU.max))
                nc.vector.tensor_scalar(wint[:, c, :], wraw[:, c, :], high[:, c:c + 1], None, ALU.min).then_inc(wint_ready, 1)
            dve.wait_ge(const_in, 32)
            nc.vector.tensor_copy(t.identb[:], t.ident[:]).then_inc(wint_ready, 1)
            for kc in range(KC):
                dve.wait_ge(wT_ps, kc + 1)
                nc.vector.tensor_copy(wT[:, kc].rearrange("k c m -> k (c m)"), psW[0:KP, kc, 0:WCH * P]).then_inc(wT_ready, 1)
                nc.vector.tensor_copy(t.wpT[:, kc, :], psW[0:KP, kc, WCH * P:WCH * P + D]).then_inc(wT_ready, 1)
            dve.wait_ge(pos_in, 16)
            for g in range(NG):
                lo, hi = g * GT, g * GT + GT
                p0 = lo % TB
                dve.wait_ge(gathered[g], 16 * 2 * GT)
                step(nc.vector.tensor_tensor(seg_rows[:, lo:hi, :], seg_rows[:, lo:hi, :], pos[:, p0:p0 + GT, :], ALU.add))
                step(nc.vector.tensor_tensor(t.h[:, lo:hi, :], seg_rows[:, lo:hi, :], tok_rows[:, lo:hi, :], ALU.add))
                layer_norm_dve(nc, dve, L, t.h, xn, g, GT)
            for g in range(NG):
                dve.wait_ge(y_ready, WCH * (g + 1))
                part = y[:, :, g * GTOK:g * GTOK + GTOK]
                nc.vector.tensor_reduce(yext[:, 0, g, :], part, AX, ALU.max).then_inc(y_ext, 1)
                nc.vector.tensor_reduce(yext[:, 1, g, :], part, AX, ALU.min, negate=True).then_inc(y_ext, 1)
            dve.wait_ge(y_ext, 2 * NG)
            for i in range(2):
                nc.vector.tensor_reduce(ymm[:, i:i + 1], yext[:, i].rearrange("p g c -> p (g c)"), AX, ALU.max).then_inc(ymm_ready, 1)
            dve.wait_ge(ymm_all, 1)
            quant_params_dve(nc, step, t.yall[:], t.ypar[:])
            inv, high = t.ypar[:, 1:2], t.ypar[:, 3:4]

            def quantise(dst, c):
                step(nc.vector.tensor_scalar(y[:, c, :], y[:, c, :], inv, ROUND, ALU.mult, ALU.add))
                return nc.vector.tensor_scalar(dst, y[:, c, :], ROUND, high, ALU.subtract, ALU.min)

            for c in range(2):
                quantise(vint[:, c, :], 4 + c).then_inc(vint_ready, 1)
            for c in range(2):
                step(quantise(t.kf[:, c, :], 2 + c))
            qint = y[:, 5, :].bitcast(BF16)
            dve.wait_ge(vint_ready, 2)
            for c in range(2):
                step(quantise(qint[:, c * TOK:c * TOK + TOK], c))
            for h in range(HEADS):
                c = h // HPC
                last = nc.vector.tensor_scalar(t.qm[:, h, :], qint[:, c * TOK:c * TOK + TOK],
                                               t.headmask[:, h:h + 1], None, ALU.mult)
            step(last)

        @block.scalar
        def _(act):
            def to_xT(g):
                for kc in range(KC):
                    act.wait_ge(xT_ps, KC * g + kc + 1)
                    nc.scalar.copy(xT[:, kc, g * GTOK:g * GTOK + GTOK], psT[0:KP, kc, :]).then_inc(xT_ready, 1)

            def to_y(g):
                for c in range(WCH):
                    n = WCH * g + c
                    act.wait_ge(y_ps, n + 1)
                    nc.scalar.activation(y[:, c, g * GTOK:g * GTOK + GTOK], psY[:, n % 4, :], ACT.Identity,
                                         bias=bias[:, c:c + 1], scale=t.wscale[:, c:c + 1]).then_inc(y_ready, 1)

            act.wait_ge(bias_in, 16 * 6)
            layer_norm_act(nc, act, L, 0, GT)
            for g in range(NG):
                to_xT(g)
                if g + 1 < NG:
                    layer_norm_act(nc, act, L, g + 1, GT)
                to_y(g)
            for b in range(4):
                act.wait_ge(v_ps, b + 1)
                src = psW[:, b % 2, :].rearrange("p (n d) -> p n d", d=2 * P)
                nc.scalar.copy(t.v[:, b * 4:b * 4 + 4, :], src[:, :, 0:D]).then_inc(v_ready, 1)

        @block.tensor
        def _(pe):
            pe.wait_ge(wint_ready, WCH + 3)
            for kc in range(KC):
                for c in range(WCH + 2):
                    mm = nc.tensor.transpose(psW[0:KP, kc, c * P:c * P + P], wint[:, c, kc * KP:kc * KP + KP], t.identb[:])
                mm.then_inc(wT_ps, 1)
            for g in range(NG):
                for kc in range(KC):
                    if g >= 1:
                        pe.wait_ge(xT_ready, KC * (g - 1) + kc + 1)
                    for i in range(GT):
                        pe.wait_ge(L.normed, g * GT + i + 1)
                        mm = nc.tensor.transpose(psT[0:KP, kc, i * P:i * P + P], xn[:, g * GT + i, kc * KP:kc * KP + KP],
                                                 t.ident[:])
                    mm.then_inc(xT_ps, 1)
                pe.wait_ge(xT_ready, KC * (g + 1))
                pe.wait_ge(wT_ready, 2 * KC)
                for c in range(WCH):
                    n = WCH * g + c
                    if n >= 4:
                        pe.wait_ge(y_ready, n - 3)
                    for kc in range(KC):
                        mm = nc.tensor.matmul(psY[:, n % 4, :], wT[:, kc, c, :], xT[:, kc, g * GTOK:g * GTOK + GTOK],
                                              start=(kc == 0), stop=(kc == KC - 1))
                    mm.then_inc(y_ps, 1)
            pe.wait_ge(vint_ready, 2)
            for b in range(4):
                if b >= 2:
                    pe.wait_ge(v_ready, b - 1)
                for i in range(4):
                    tile = b * 4 + i
                    for c in range(2):
                        o = i * 2 * P + c * P
                        mm = nc.tensor.transpose(psW[:, b % 2, o:o + P], vint[:, c, tile * P:tile * P + P], t.identb[:])
                mm.then_inc(v_ps, 1)


def score_extremes(nc, t):
    with ExitStack() as ctx:
        def sem(name):
            return ctx.enter_context(nc.semaphore(name))

        SLOTS = 4
        scores = ctx.enter_context(nc.psum_tensor("x_scores", [P, SLOTS, S], F32))
        rowmin = ctx.enter_context(nc.sbuf_tensor("rowmin", [P, NT * HEADS], F32))
        smm = ctx.enter_context(nc.sbuf_tensor("smm", [P, 2], F32))
        sall = ctx.enter_context(nc.sbuf_tensor("sall", [P, 2], F32))
        spar = ctx.enter_context(nc.sbuf_tensor("spar", [P, 4], F32))
        w = ctx.enter_context(nc.sbuf_tensor("softmax_tmp", [P, 8], F32))
        HALF_S = S // 2
        kneg = ctx.enter_context(nc.sbuf_tensor("kneg", [P, 2, B * HALF_S], BF16))
        apart = ctx.enter_context(nc.sbuf_tensor("apart", [P, SLOTS, HALF_S], F32))
        larger = ctx.enter_context(nc.sbuf_tensor("larger", [P, 2, HALF_S], F32))
        smaller = ctx.enter_context(nc.sbuf_tensor("smaller", [P, 2, HALF_S], F32))
        tile_max = ctx.enter_context(nc.sbuf_tensor("tile_max", [P, HEADS], F32))
        tile_min = ctx.enter_context(nc.sbuf_tensor("tile_min", [P, HEADS], F32))
        kneg_ready, scores_ready, scores_used, apart_ready, max_done, tile_kept, fold_starts = (
            sem(n) for n in ("kneg_ready", "x_scores_ready", "x_scores_used", "apart_ready", "max_done", "tile_kept", "fold_starts"))
        smm_ready, smm_all, dve_step = sem("smm_ready"), sem("smm_all"), sem("x_dve_step")
        block = ctx.enter_context(nc.Block())

        @block.gpsimd
        def _(pool):
            for c in range(2):
                for b in range(B):
                    nc.gpsimd.tensor_scalar(kneg[:, c, b * HALF_S:b * HALF_S + HALF_S],
                                            t.kf[:, c, b * S + HALF_S:b * S + S], -1.0, 0.0, ALU.mult,
                                            ALU.add).then_inc(kneg_ready, 1)
                    pool.wait_ge(kneg_ready, c * B + b + 1)
            pool.wait_ge(smm_ready, 2)
            nc.gpsimd.partition_all_reduce(sall[:], smm[:], P, RMAX).then_inc(smm_all, 1)

        @block.tensor
        def _(pe):
            def row_tile(i, first):
                batch = i // TB
                for h in range(HEADS):
                    if not (first and h < SLOTS):
                        pe.wait_ge(scores_used, i * HEADS + (h + 1 - SLOTS))
                    q, c = t.qm[:, h, bass.ds(i * P, P)], h // HPC
                    left = t.kf[:, c, bass.ds(batch * S, HALF_S)]
                    for j, right in enumerate((t.kf[:, c, bass.ds(batch * S + HALF_S, HALF_S)],
                                               kneg[:, c, bass.ds(batch * HALF_S, HALF_S)])):
                        dst = scores[:, h % SLOTS, j * HALF_S:j * HALF_S + HALF_S]
                        nc.tensor.matmul(dst, q, left, start=True, stop=False)
                        mm = nc.tensor.matmul(dst, q, right, start=False, stop=True)
                    mm.then_inc(scores_ready, 1)

            pe.wait_ge(kneg_ready, 2 * B)
            row_tile(0, True)
            with pe.Fori(1, NT) as i:
                row_tile(i, False)

        @block.scalar
        def _(act):
            def row_tile(i, first):
                for h in range(HEADS):
                    n = i * HEADS + h
                    if not (first and h < SLOTS):
                        act.wait_ge(scores_used, n + 1 - SLOTS)
                    act.wait_ge(scores_ready, n + 1)
                    nc.scalar.activation(apart[:, h % SLOTS, :], scores[:, h % SLOTS, HALF_S:S], ACT.Abs).then_inc(apart_ready, 1)

            row_tile(0, True)
            with act.Fori(1, NT) as i:
                row_tile(i, False)

        @block.vector
        def _(dve):
            def row_tile(i, first):
                for h in range(HEADS):
                    n = i * HEADS + h
                    dve.wait_ge(apart_ready, n + 1)
                    if not (first and h < 2):
                        dve.wait_ge(scores_used, n - 1)
                    dve.sem_inc(fold_starts, 1)
                    both, gap = scores[:, h % SLOTS, 0:HALF_S], apart[:, h % SLOTS, :]
                    nc.vector.tensor_tensor_reduce(larger[:, h % 2], both, gap, 1.0, -BIG, ALU.add, ALU.max,
                                                   tile_max[:, h:h + 1]).then_inc(max_done, 1)
                    nc.vector.tensor_tensor_reduce(smaller[:, h % 2], gap, both, 1.0, -BIG, ALU.subtract, ALU.max,
                                                   tile_min[:, h:h + 1]).then_inc(scores_used, 1)
                dve.wait_ge(max_done, (i + 1) * HEADS)
                dve.wait_ge(scores_used, (i + 1) * HEADS)
                nc.vector.tensor_copy(t.rowmax[:, bass.ds(i * HEADS, HEADS)], tile_max[:]).then_inc(tile_kept, 1)
                nc.vector.tensor_copy(rowmin[:, bass.ds(i * HEADS, HEADS)], tile_min[:]).then_inc(tile_kept, 1)
                dve.wait_ge(tile_kept, (i + 1) * 2)

            row_tile(0, True)
            with dve.Fori(1, NT) as i:
                row_tile(i, False)
            nc.vector.tensor_reduce(smm[:, 0:1], t.rowmax[:], AX, ALU.max).then_inc(smm_ready, 1)
            nc.vector.tensor_reduce(smm[:, 1:2], rowmin[:], AX, ALU.max).then_inc(smm_ready, 1)
            dve.wait_ge(smm_all, 1)
            step = chain_on(dve, dve_step)
            cl, c2, tmp, flo, cmp = (w[:, i:i + 1] for i in range(5))
            scale_y = t.ypar[:, 0:1]
            step(nc.vector.tensor_scalar(cl, scale_y, scale_y, float(HD) ** -0.5, ALU.mult, ALU.mult))
            step(nc.vector.tensor_scalar(sall[:], sall[:], cl, 0.5, ALU.mult, ALU.mult))
            quant_params_dve(nc, step, sall[:], spar[:])
            scale, inv, high = spar[:, 0:1], spar[:, 1:2], spar[:, 3:4]
            step(nc.vector.tensor_tensor(c2, cl, inv, ALU.mult))
            step(nc.vector.tensor_scalar(t.negc2[:], c2, -1.0, None, ALU.mult))
            step(nc.vector.tensor_scalar(t.rowmax[:], t.rowmax[:], 0.5, None, ALU.mult))
            step(nc.vector.tensor_scalar(t.rowmax[:], t.rowmax[:], c2, ROUND, ALU.mult, ALU.add))
            step(nc.vector.tensor_scalar(t.rowmax[:], t.rowmax[:], ROUND, high, ALU.subtract, ALU.min))

            def floor(dst, src, up):
                step(nc.vector.tensor_scalar(flo, src, ROUND, ROUND, ALU.add, ALU.subtract))
                step(nc.vector.tensor_tensor(cmp, flo, src, ALU.is_lt if up else ALU.is_gt))
                step(nc.vector.tensor_tensor(dst, flo, cmp, ALU.add if up else ALU.subtract))

            X, invX, qoff, Xmax, nhb, K = (t.smpar[:, i:i + 1] for i in range(6))
            b = w[:, 5:6]
            step(nc.vector.tensor_scalar(tmp, inv, X0, None, ALU.mult))
            floor(X, tmp, True)
            step(nc.vector.reciprocal(invX, X))
            step(nc.vector.tensor_scalar(qoff, invX, 0.5, -0.5, ALU.mult, ALU.add))
            step(nc.vector.tensor_scalar(Xmax, X, N_HALVINGS, None, ALU.mult))
            step(nc.vector.tensor_scalar(tmp, inv, B_NUM, None, ALU.mult))
            floor(b, tmp, False)
            step(nc.vector.tensor_scalar(nhb, b, -0.5, None, ALU.mult))
            step(nc.vector.tensor_scalar(tmp, scale, scale, None, ALU.mult))
            step(nc.vector.reciprocal(tmp, tmp))
            step(nc.vector.tensor_scalar(tmp, tmp, C_NUM, None, ALU.mult))
            floor(K, tmp, False)
            step(nc.vector.tensor_tensor(b, b, b, ALU.mult))
            step(nc.vector.scalar_tensor_tensor(out=K, in0=b, scalar=-0.25, in1=K, op0=ALU.mult, op1=ALU.add))


PAIRS = HEADS // 2
LAST = NT * PAIRS
S_SLOTS = 3


def attention(nc, t):
    with ExitStack() as ctx:
        def sb(name, shape, dt):
            return ctx.enter_context(nc.sbuf_tensor(name, shape, dt))

        def sem(name):
            return ctx.enter_context(nc.semaphore(name))

        scores = ctx.enter_context(nc.psum_tensor("scores", [P, S_SLOTS, S], F32))
        po = ctx.enter_context(nc.psum_tensor("po", [P, 512], F32))
        below = sb("below", [P, 2, 2, S], I16)
        clamped = sb("clamped", [P, 2, S], I16)
        halvings = sb("halvings", [P, 2, S], I16)
        whole = sb("whole", [P, 2, S], I16)
        rest = sb("rest", [P, 2, 2, S], I16)
        half_pow = sb("half_pow", [P, 2, 2, S], I16)
        square = sb("square", [P, 2, 2, S], F32)
        expo = sb("expo", [P, 2, 2, S], F32)
        esum = sb("esum", [P, 2, 2], F32)
        rsum = sb("rsum", [P, 2, 2], F32)
        logp = sb("logp", [P, 2, S], F32)
        ratio = sb("ratio", [P, 2, 2, S], U16)
        power = sb("power", [P, 2, S], BF16)
        probs = sb("probs", [P, 2, 2, S], U16)
        probsT = sb("probsT", [P, 2, 2 * TB, P], BF16)
        scores_ready, below_ready, clamped_ready, whole_ready, rest_ready = (
            sem(n) for n in ("scores_ready", "below_ready", "clamped_ready", "whole_ready", "rest_ready"))
        halv_ready, pow_ready, square_ready, expo_ready, rsum_ready, logp_ready, ratio_ready = (
            sem(n) for n in ("halv_ready", "pow_ready", "square_ready", "expo_ready", "rsum_ready", "logp_ready", "ratio_ready"))
        power_ready, probs_ready, pv_ready, out_ready = (
            sem(n) for n in ("power_ready", "probs_ready", "pv_ready", "out_ready"))
        turn_starts, below_starts = sem("turn_starts"), sem("below_starts")
        turned = [sem(f"turned{s}") for s in range(2)]
        block = ctx.enter_context(nc.Block())
        X, invX, qoff, Xmax, nhb, K = (t.smpar[:, i:i + 1] for i in range(6))

        def pair_at(i, g, lag):
            row, p = (i, g - lag) if g >= lag else (i - 1, g - lag + PAIRS)
            if type(i) is int and not 0 <= row < NT:
                return None
            return row, p

        def steps(eng, body):
            for g in range(PAIRS):
                body(0, g)
            with eng.Fori(1, NT) as i:
                for g in range(PAIRS):
                    body(i, g)
            for g in range(PAIRS):
                body(NT, g)

        def after(row, p, n):
            return row * PAIRS + (p + 1 + n)

        def exists(row, p, n):
            return type(row) is not int or row * PAIRS + p >= n

        @block.tensor
        def _(pe):
            def make_scores(row, p):
                for h in (2 * p, 2 * p + 1):
                    if exists(row, p, 2) or h >= S_SLOTS:
                        pe.wait_ge(below_ready, row * HEADS + (h + 1 - S_SLOTS))
                    for j in range(S // 512):
                        mm = nc.tensor.matmul(scores[:, h % S_SLOTS, j * 512:j * 512 + 512],
                                              t.qm[:, h, bass.ds(row * P, P)],
                                              t.kf[:, h // HPC, bass.ds((row // TB) * S + j * 512, 512)],
                                              start=True, stop=True)
                    mm.then_inc(scores_ready, 1)

            def times_v(row, p):
                pe.wait_ge(turned[p % 2], (row * (PAIRS // 2) + (p // 2 + 1)) * 16)
                if p == 0 and exists(row, p, PAIRS):
                    pe.wait_ge(out_ready, row * 3)
                for h in (2 * p, 2 * p + 1):
                    for m in range(TB):
                        mm = nc.tensor.matmul(po[:, h * HD:h * HD + HD], probsT[:, p % 2, (h % 2) * TB + m, :],
                                              t.v[:, bass.ds((row // TB) * TB + m, 1), h * HD:h * HD + HD],
                                              start=(m == 0), stop=(m == TB - 1))
                mm.then_inc(pv_ready, 1)

            def body(i, g):
                if at := pair_at(i, g, 0):
                    make_scores(*at)
                if at := pair_at(i, g, 6):
                    times_v(*at)

            steps(pe, body)

        @block.scalar
        def _(act):
            nc.scalar.preload_act_table_set("natural_log_exp_and_others")

            def make_below(row, p):
                if exists(row, p, 2):
                    act.wait_ge(clamped_ready, after(row, p, -2))
                for h in (2 * p, 2 * p + 1):
                    act.wait_ge(scores_ready, row * HEADS + (h + 1))
                    act.sem_inc(below_starts, 1)
                    nc.scalar.activation(below[:, p % 2, h % 2, :], scores[:, h % S_SLOTS, :], ACT.Relu,
                                         bias=t.rowmax[:, bass.ds(row * HEADS + h, 1)], scale=t.negc2[:]).then_inc(below_ready, 1)

            def make_log(row, p):
                act.wait_ge(rsum_ready, after(row, p, 0))
                if exists(row, p, 1):
                    act.wait_ge(ratio_ready, after(row, p, -1))
                for h in range(2):
                    nc.scalar.activation(logp[:, h, :], expo[:, p % 2, h, :], ACT.Ln,
                                         scale=rsum[:, p % 2, h:h + 1]).then_inc(logp_ready, 1)

            def make_ratio(row, p):
                act.wait_ge(logp_ready, after(row, p, 0) * 2)
                if exists(row, p, 2):
                    act.wait_ge(power_ready, after(row, p, -2))
                nc.scalar.activation(ratio[:, p % 2], logp[:], ACT.Exp, scale=-1.0).then_inc(ratio_ready, 1)

            def make_square(row, p):
                act.wait_ge(rest_ready, after(row, p, 0))
                if exists(row, p, 2):
                    act.wait_ge(expo_ready, after(row, p, -2) * 2)
                nc.scalar.activation(square[:, p % 2], rest[:, p % 2], ACT.Square, bias=nhb).then_inc(square_ready, 1)

            def body(i, g):
                if at := pair_at(i, g, 0):
                    make_below(*at)
                if at := pair_at(i, g, 3):
                    make_log(*at)
                if at := pair_at(i, g, 1):
                    make_square(*at)
                if at := pair_at(i, g, 3):
                    make_ratio(*at)

            steps(act, body)

        @block.vector
        def _(dve):
            def power_of(row, p):
                dve.wait_ge(ratio_ready, after(row, p, 0))
                if exists(row, p, 1):
                    dve.wait_ge(probs_ready, after(row, p, -1))
                nc.vector.tensor_scalar(power[:], ratio[:, p % 2], POW2 * POW_SHIFT, POW_LIMIT,
                                        ALU.mult, ALU.min).then_inc(power_ready, 1)

            def probs_of(row, p):
                dve.wait_ge(power_ready, after(row, p, 0))
                if exists(row, p, 2):
                    dve.wait_ge(pv_ready, after(row, p, -2))
                nc.vector.tensor_scalar(probs[:, p % 2], power[:].bitcast(U16), EXP_MASK, POW_FLIP,
                                        ALU.bitwise_and, ALU.bitwise_xor).then_inc(probs_ready, 1)

            def clamped_of(row, p):
                dve.wait_ge(below_ready, row * HEADS + (2 * p + 2))
                if exists(row, p, 1):
                    dve.wait_ge(rest_ready, after(row, p, -1))
                nc.vector.tensor_scalar(clamped[:], below[:, p % 2], Xmax, None, ALU.min).then_inc(clamped_ready, 1)

            def halvings_of(row, p):
                dve.wait_ge(clamped_ready, after(row, p, 0))
                if exists(row, p, 1):
                    dve.wait_ge(pow_ready, after(row, p, -1))
                nc.vector.tensor_scalar(halvings[:], clamped[:], invX, qoff, ALU.mult, ALU.add).then_inc(halv_ready, 1)

            def whole_of(row, p):
                dve.wait_ge(halv_ready, after(row, p, 0))
                nc.vector.tensor_scalar(whole[:], halvings[:], X, None, ALU.mult).then_inc(whole_ready, 1)

            def half_pow_of(row, p):
                if exists(row, p, 2):
                    dve.wait_ge(expo_ready, after(row, p, -2) * 2)
                nc.vector.tensor_scalar(half_pow[:, p % 2], halvings[:], -128.0, 127.0 * 128.0,
                                        ALU.mult, ALU.add).then_inc(pow_ready, 1)

            def rest_of(row, p):
                dve.wait_ge(whole_ready, after(row, p, 0))
                if exists(row, p, 2):
                    dve.wait_ge(square_ready, after(row, p, -2))
                nc.vector.tensor_tensor(rest[:, p % 2], clamped[:], whole[:], ALU.subtract).then_inc(rest_ready, 1)

            def expo_of(row, p):
                dve.wait_ge(square_ready, after(row, p, 0))
                dve.wait_ge(pow_ready, after(row, p, 0))
                if exists(row, p, 2):
                    dve.wait_ge(logp_ready, after(row, p, -2) * 2)
                for h in range(2):
                    nc.vector.scalar_tensor_tensor(
                        out=expo[:, p % 2, h, :], in0=square[:, p % 2, h, :], scalar=K,
                        in1=half_pow[:, p % 2, h, :].bitcast(BF16), op0=ALU.add, op1=ALU.mult,
                        accum_out=esum[:, p % 2, h:h + 1]).then_inc(expo_ready, 1)

            def rsum_of(row, p):
                dve.wait_ge(expo_ready, after(row, p, 0) * 2)
                nc.vector.reciprocal(rsum[:, p % 2, :], esum[:, p % 2, :]).then_inc(rsum_ready, 1)

            def copy_out(row):
                dve.wait_ge(pv_ready, row * PAIRS + PAIRS)
                nc.vector.tensor_scalar(t.o[:, bass.ds(row, 1), :], po[:, 0:D].unsqueeze(1), 2.0 ** PSHIFT, t.ypar[:, 0:1],
                                        ALU.mult, ALU.mult).then_inc(out_ready, 1)
                nc.vector.tensor_reduce(t.omax[:, bass.ds(row, 1)], po[:, 0:D], AX, ALU.max).then_inc(out_ready, 1)
                nc.vector.tensor_reduce(t.onmin[:, bass.ds(row, 1)], po[:, 0:D], AX, ALU.min, negate=True).then_inc(out_ready, 1)

            ORDER = ((power_of, 5), (clamped_of, 1), (probs_of, 5), (halvings_of, 1), (expo_of, 2),
                     (whole_of, 1), (rsum_of, 2), (half_pow_of, 1), (rest_of, 1))

            def body(i, g):
                for work, lag in ORDER:
                    if at := pair_at(i, g, lag):
                        work(*at)
                if g == PAIRS - 1 and (at := pair_at(i, g, PAIRS)):
                    copy_out(at[0])

            steps(dve, body)

        @block.sync
        def _(sp):
            def turn(row, p):
                sp.wait_ge(probs_ready, after(row, p, 0))
                sp.sem_inc(turn_starts, 1)
                sp.dma_start_transpose(probsT[:, p % 2], probs[:, p % 2].rearrange("p h m -> p (h m)").bitcast(BF16)
                                       ).then_inc(turned[p % 2], 16)

            def body(i, g):
                if at := pair_at(i, g, 4):
                    turn(*at)

            steps(sp, body)


class Prepared:

    def __init__(self, sb, sem):
        self.raw1 = sb("raw1", [P, 2, WCHUNKS, H], F32)
        self.raw2 = sb("raw2", [P, 2, HC, D], F32)
        self.w1 = sb("w1_parts", [P, 2, WCHUNKS, H], F16)
        self.w2 = sb("w2_parts", [P, 2, HC, 2, D], F16)
        self.b1 = sb("b1c", [P, E * HC], F32)
        self.junk = sb("squares", [P, WCHUNKS * H], BF16)
        self.sums = sb("square_sums", [P, 2, 2], F32)
        self.b1sum = sb("b1_square_sum", [P, 1], F32)
        self.total = sb("total_sums", [P, 2, 3], F32)
        self.b1total = sb("b1_total", [P, 1], F32)
        self.power = sb("norm_powers", [P, 2, 3], F32)
        self.mult = sb("weight_scales", [P, 2, 3], F32)
        self.undo = sb("scales_undone", [P, 2, 2], F32)
        self.raw_in = [sem(f"raw_in{s}") for s in range(2)]
        self.b1_in, self.b1_summed = sem("b1_in"), sem("b1_summed")
        self.summed, self.scaled, self.hi_ready, self.lo_ready, self.scale_step, self.totalled, self.total_starts = (
            sem(n) for n in ("w_summed", "w_scaled", "w_hi_ready", "w_lo_ready", "w_scale_step", "w_totalled", "w_total_starts"))


def load_expert(nc, sp, W, io, e, slot):
    w1 = io.w1[bass.ds(e, 1)].rearrange("e k h -> k (e h)")
    for dst, src in ((W.raw1[:, slot, 0, :], w1[0:P]), (W.raw1[0:HALF, slot, 1, :], w1[P:D]),
                     (W.raw1[HALF:P, slot, 1, :], w1[0:HALF]), (W.raw1[:, slot, 2, :], w1[HALF:D]),
                     (W.raw2[:, slot], io.w2[bass.ds(e, 1)].rearrange("e (j k) d -> k (e j) d", k=P))):
        sp.dma_start(dst, src).then_inc(W.raw_in[slot], 16)


RAW_IN = 5 * 16


def square_sums_act(nc, act, W, n, slot, k):
    act.wait_ge(W.raw_in[slot], (k + 1) * RAW_IN)
    for i, raw in enumerate((W.raw1[:, slot].rearrange("p c h -> p (c h)"), W.raw2[:, slot].rearrange("p j d -> p (j d)"))):
        if type(n) is not int or n > 0 or i > 0:
            act.wait_ge(W.summed, n * 2 + i)
        nc.scalar.activation(W.junk[:, 0:raw.shape[1]], raw, ACT.Square, accum_out=W.sums[:, slot, i:i + 1]).then_inc(W.summed, 1)


def total_sums_pool(nc, pool, W, n, slot):
    pool.wait_ge(W.summed, n * 2 + 2)
    pool.sem_inc(W.total_starts, 1)
    nc.gpsimd.partition_all_reduce(W.total[:, slot, 0:2], W.sums[:, slot], P, RADD).then_inc(W.totalled, 1)


def power_below(nc, step, power, mult, total):
    step(nc.vector.tensor_scalar(total, total, 1e-30, None, ALU.add))
    step(nc.vector.tensor_scalar(power.bitcast(U32), total.bitcast(U32), 1, EXP_BITS,
                                 ALU.logical_shift_right, ALU.bitwise_and))
    step(nc.vector.tensor_scalar(mult.bitcast(U32), power.bitcast(U32), EXP_BITS, None, ALU.bitwise_xor))
    step(nc.vector.tensor_scalar(mult, mult, 2.0 ** (15 - 66), None, ALU.mult))


SCALE_STEPS = 6


def scales_dve(nc, dve, W, n, slot):
    count = [0]

    def step(ins):
        ins.then_inc(W.scale_step, 1)
        count[0] += 1
        dve.wait_ge(W.scale_step, n * SCALE_STEPS + count[0])

    total, power, mult, undo = W.total[:, slot], W.power[:, slot], W.mult[:, slot], W.undo[:, slot]
    dve.wait_ge(W.totalled, n + 1)
    step(nc.vector.tensor_scalar(total[:, 2:3], total[:, 0:1], float(D), W.b1total[:], ALU.mult, ALU.add))
    power_below(nc, step, power, mult, total)
    nc.vector.tensor_scalar(undo[:, 0:1], power[:, 0:1], 2.0 ** 50 / X_SCALE, None, ALU.mult).then_inc(W.scaled, 1)
    step(nc.vector.tensor_scalar(power[:, 1:3], power[:, 1:3], 2.0 ** 50, None, ALU.mult))
    nc.vector.tensor_tensor(undo[:, 1:2], power[:, 1:2], power[:, 2:3], ALU.mult).then_inc(W.scaled, 1)


def high_parts_act(nc, act, W, n, slot):
    act.wait_ge(W.scaled, n * 2 + 2)
    nc.scalar.activation(W.w1[:, slot], W.raw1[:, slot], ACT.Copy, scale=W.mult[:, slot, 0:1]).then_inc(W.hi_ready, 1)
    nc.scalar.activation(W.w2[:, slot, :, 0, :], W.raw2[:, slot], ACT.Copy, scale=W.mult[:, slot, 1:2]).then_inc(W.hi_ready, 1)


def low_parts_dve(nc, dve, W, n, slot):
    dve.wait_ge(W.hi_ready, n * 2 + 2)
    for p0, raw, hi, lo, i in ((0, W.raw1[:, slot, 2, :], W.w1[:, slot, 2, :], W.w1[:, slot, 2, :], 0),
                               (HALF, W.raw1[HALF:P, slot, 1, :], W.w1[HALF:P, slot, 1, :], W.w1[HALF:P, slot, 1, :], 0),
                               (0, W.raw2[:, slot], W.w2[:, slot, :, 0, :], W.w2[:, slot, :, 1, :], 1)):
        nc.vector.scalar_tensor_tensor(out=lo, in0=raw, scalar=W.mult[p0:P, slot, i:i + 1], in1=hi, op0=ALU.mult,
                                       op1=ALU.subtract).then_inc(W.lo_ready, 1)


def project_and_route(nc, t, io):
    with ExitStack() as ctx:
        def sb(name, shape, dt):
            return ctx.enter_context(nc.sbuf_tensor(name, shape, dt))

        def sem(name):
            return ctx.enter_context(nc.semaphore(name))

        oext, oall, opar = sb("oext", [P, 2], F32), sb("oall", [P, 2], F32), sb("opar", [P, 4], F32)
        oint = sb("oint", [P, NT, D], BF16)
        oT = sb("oT", [KP, KC, TOK], BF16)
        ones = sb("ones", [P, P], F32)
        diag = sb("diag", [P, 2, P], F32)
        srow = sb("srow", [P, D], F32)
        brow = sb("brow", [P, D], F32)
        p = sb("p_out", [P, NT, D], F32)
        pext, pall, ppar = sb("pext", [P, 2], F32), sb("pall", [P, 2], F32), sb("ppar", [P, 4], F32)
        graw = sb("graw", [P, WCHUNKS, E], F32)
        gparts = sb("gparts", [P, WCHUNKS, E], F16)
        gsum, gtotal = sb("gsum", [P, 2], F32), sb("gtotal", [P, 2], F32)
        gpow, gmult = sb("gpow", [P, 1], F32), sb("gmult", [P, 1], F32)
        xs = sb("x_parts", [P, NT, XCH * P], F16)
        identh = sb("identh", [P, P], F16)
        psT = ctx.enter_context(nc.psum_tensor("r_psT", [P, 2, 1024], F16))
        psO = ctx.enter_context(nc.psum_tensor("psO", [P, 2, 1024], BF16))
        psP = ctx.enter_context(nc.psum_tensor("psP", [P, 2, 512], F32))
        psR = ctx.enter_context(nc.psum_tensor("psR", [P, 512], F32))
        psG = ctx.enter_context(nc.psum_tensor("psG", [P, 512], F32))
        xn = p
        L = Norm(sb, sem, "norm2")
        W = t.W
        g_summed, g_totalled, g_scaled, g_hi_ready, g_lo_ready, x_hi_ready, x_lo_ready, zeros_ready, identh_ready = (
            sem(n) for n in ("g_summed", "g_totalled", "g_scaled", "g_hi_ready", "g_lo_ready", "x_hi_ready", "x_lo_ready",
                             "zeros_ready", "identh_ready"))
        rows_in, gate_in, dve_step, oext_ready, oall_ready, oint_ready, ones_ready, diag_ready, srow_ps = (
            sem(n) for n in ("rows_in", "gate_in", "r_dve_step", "oext_ready", "oall_ready", "oint_ready", "ones_ready",
                             "diag_ready", "srow_ps"))
        oT_ps, oT_ready, p_ps, p_used, pext_ready, pall_ready, xT_ps, xT_ready, gate_ps = (
            sem(n) for n in ("oT_ps", "oT_ready", "p_ps", "p_used", "pext_ready", "pall_ready", "r_xT_ps", "r_xT_ready",
                             "gate_ps"))
        block = ctx.enter_context(nc.Block())

        @block.sync
        def _(sp):
            sp.dma_start(brow[:], io.b_proj.partition_broadcast(P)).then_inc(rows_in, 16)
            with nc.allow_non_contiguous_dma("gate weights, transposed"):
                gate = io.gate_w.rearrange("e k -> k e")
                for dst, src in ((graw[:, 0, :], gate[0:P]), (graw[0:HALF, 1, :], gate[P:D]),
                                 (graw[HALF:P, 1, :], gate[0:HALF]), (graw[:, 2, :], gate[HALF:D])):
                    sp.dma_start(dst, src).then_inc(gate_in, 16)
                sp.dma_start(W.b1[:], io.b1.rearrange("e (j p) -> p (e j)", p=P)).then_inc(W.b1_in, 16)
            for n in range(2):
                load_expert(nc, sp, W, io, n, n)

        @block.gpsimd
        def _(pool):
            nc.gpsimd.memset(ones[:], 1.0).then_inc(ones_ready, 1)
            nc.gpsimd.memset(xs[:, :, 3 * D:XCH * P], 0.0).then_inc(zeros_ready, 1)
            pool.wait_ge(oext_ready, 1)
            nc.gpsimd.partition_all_reduce(oall[:], oext[:], P, RMAX).then_inc(oall_ready, 1)
            pool.wait_ge(g_summed, 2)
            nc.gpsimd.partition_all_reduce(gtotal[:], gsum[:], P, RADD).then_inc(g_totalled, 1)
            total_sums_pool(nc, pool, W, 0, 0)
            pool.wait_ge(pext_ready, 2)
            nc.gpsimd.partition_all_reduce(pall[:], pext[:], P, RMAX).then_inc(pall_ready, 1)

        @block.vector
        def _(dve):
            step = L.chain = chain_on(dve, dve_step)
            flat_p = p[:].rearrange("p r d -> p (r d)")
            step(nc.vector.tensor_reduce(oext[:, 0:1], t.omax[:], AX, ALU.max))
            step(nc.vector.tensor_reduce(oext[:, 1:2], t.onmin[:], AX, ALU.max))
            nc.vector.tensor_scalar(oext[:], oext[:], 2.0 ** PSHIFT, t.ypar[:, 0:1], ALU.mult, ALU.mult).then_inc(oext_ready, 1)
            nc.vector.tensor_copy(identh[:], t.ident[:]).then_inc(identh_ready, 1)
            for c in range(2):
                nc.vector.tensor_scalar(diag[:, c, :], t.ident[:], t.wscale[:, WCH + c:WCH + c + 1], None,
                                        ALU.mult).then_inc(diag_ready, 1)
            dve.wait_ge(oall_ready, 1)
            quant_params_dve(nc, step, oall[:], opar[:])
            for g in range(NG):
                part = t.o[:, g * GT:g * GT + GT, :]
                step(nc.vector.tensor_scalar(part, part, opar[:, 1:2], ROUND, ALU.mult, ALU.add))
                nc.vector.tensor_scalar(oint[:, g * GT:g * GT + GT, :], part, ROUND, opar[:, 3:4],
                                        ALU.subtract, ALU.min).then_inc(oint_ready, 1)
            dve.wait_ge(g_totalled, 1)
            power_below(nc, step, gpow[:], gmult[:], gtotal[:, 0:1])
            nc.vector.tensor_scalar(t.gundo[:], gpow[:], 2.0 ** 50 / X_SCALE, None, ALU.mult).then_inc(g_scaled, 1)
            step(nc.vector.tensor_scalar(W.b1total[:], gtotal[:, 1:2], 2.0, None, ALU.mult))
            dve.wait_ge(g_hi_ready, 1)
            for p0, c in ((0, 2), (HALF, 1)):
                nc.vector.scalar_tensor_tensor(out=gparts[p0:P, c, :], in0=graw[p0:P, c, :], scalar=gmult[p0:P], in1=gparts[p0:P, c, :],
                                               op0=ALU.mult, op1=ALU.subtract).then_inc(g_lo_ready, 1)
            dve.wait_ge(srow_ps, 1)
            step(nc.vector.tensor_copy(srow[:], psR[:, 0:D]))
            dve.wait_ge(rows_in, 16)
            for b in range(NT // 2):
                dve.wait_ge(p_ps, b + 1)
                dst = p[:, 2 * b:2 * b + 2, :]
                src = psP[:, b % 2, 0:2 * D].rearrange("p (r d) -> p r d", r=2)
                nc.vector.scalar_tensor_tensor(out=dst, in0=src, scalar=opar[:, 0:1],
                                               in1=srow[:].unsqueeze(1).broadcast_to([P, 2, D]),
                                               op0=ALU.mult, op1=ALU.mult).then_inc(p_used, 1)
                dve.wait_ge(p_used, b + 1)
                step(nc.vector.tensor_tensor(dst, dst, brow[:].unsqueeze(1).broadcast_to([P, 2, D]), ALU.add))
            nc.vector.tensor_reduce(pext[:, 0:1], flat_p, AX, ALU.max).then_inc(pext_ready, 1)
            nc.vector.tensor_reduce(pext[:, 1:2], flat_p, AX, ALU.min, negate=True).then_inc(pext_ready, 1)
            scales_dve(nc, dve, W, 0, 0)
            dve.wait_ge(pall_ready, 1)
            quant_params_dve(nc, step, pall[:], ppar[:])
            def low_part(g):
                lo, hi = g * GT, g * GT + GT
                dve.wait_ge(x_hi_ready, g + 1)
                nc.vector.scalar_tensor_tensor(out=xs[:, lo:hi, 2 * D:3 * D], in0=xn[:, lo:hi, :], scalar=X_SCALE,
                                               in1=xs[:, lo:hi, 0:D], op0=ALU.mult, op1=ALU.subtract).then_inc(x_lo_ready, 1)

            for g in range(NG):
                lo, hi = g * GT, g * GT + GT
                part = p[:, lo:hi, :]
                step(nc.vector.tensor_scalar(part, part, ppar[:, 1:2], ROUND, ALU.mult, ALU.add))
                step(nc.vector.tensor_scalar(part, part, ROUND, ppar[:, 3:4], ALU.subtract, ALU.min))
                step(nc.vector.scalar_tensor_tensor(out=t.h[:, lo:hi, :], in0=part, scalar=ppar[:, 0:1],
                                                    in1=t.h[:, lo:hi, :], op0=ALU.mult, op1=ALU.add))
                if g >= 1:
                    low_part(g - 1)
                layer_norm_dve(nc, dve, L, t.h, xn, g, GT)
            low_parts_dve(nc, dve, W, 0, 0)
            low_part(NG - 1)

        @block.scalar
        def _(act):
            act.wait_ge(gate_in, 64)
            nc.scalar.activation(W.junk[:, 0:WCHUNKS * E], graw[:].rearrange("p c e -> p (c e)"), ACT.Square,
                                 accum_out=gsum[:, 0:1]).then_inc(g_summed, 1)
            act.wait_ge(W.b1_in, 16)
            act.wait_ge(g_summed, 1)
            nc.scalar.activation(W.junk[:, 0:E * HC], W.b1[:], ACT.Square, accum_out=gsum[:, 1:2]).then_inc(g_summed, 1)
            for g in range(NG):
                if g == 1:
                    act.wait_ge(g_scaled, 1)
                    nc.scalar.activation(gparts[:], graw[:], ACT.Copy, scale=gmult[:]).then_inc(g_hi_ready, 1)
                for kc in range(KC):
                    act.wait_ge(oT_ps, KC * g + kc + 1)
                    nc.scalar.copy(oT[:, kc, g * GTOK:g * GTOK + GTOK], psO[0:KP, kc, 0:GTOK]).then_inc(oT_ready, 1)
            act.wait_ge(g_summed, 2)
            square_sums_act(nc, act, W, 0, 0, 0)
            high_parts_act(nc, act, W, 0, 0)
            layer_norm_act(nc, act, L, 0, GT)
            for g in range(NG):
                act.wait_ge(L.normed, g * GT + GT)
                part = xs[:, g * GT:g * GT + GT, 0:2 * D].rearrange("p r (c d) -> p r c d", c=2)
                nc.scalar.activation(part, xn[:, g * GT:g * GT + GT, :].unsqueeze(2).broadcast_to([P, GT, 2, D]),
                                     ACT.Copy, scale=X_SCALE).then_inc(x_hi_ready, 1)
                if g + 1 < NG:
                    layer_norm_act(nc, act, L, g + 1, GT)
                for c in range(XCH):
                    act.wait_ge(xT_ps, XCH * g + c + 1)
                    nc.scalar.copy(t.xT[:, c, g * GTOK:g * GTOK + GTOK], psT[:, (XCH * g + c) % 2, 0:GTOK]).then_inc(xT_ready, 1)
            act.wait_ge(gate_ps, NT)
            nc.scalar.copy(t.logits[:], psG[:, 0:NT * E])

        @block.tensor
        def _(pe):
            pe.wait_ge(ones_ready, 1)
            pe.wait_ge(diag_ready, 2)
            nc.tensor.matmul(psR[:, 0:P], ones[:], diag[:, 0, :], start=True, stop=True)
            nc.tensor.matmul(psR[:, P:D], ones[:], diag[:, 1, 0:D - P], start=True, stop=True).then_inc(srow_ps, 1)
            for g in range(NG):
                pe.wait_ge(oint_ready, g + 1)
                for kc in range(KC):
                    if g >= 1:
                        pe.wait_ge(oT_ready, KC * (g - 1) + kc + 1)
                    for i in range(GT):
                        mm = nc.tensor.transpose(psO[0:KP, kc, i * P:i * P + P],
                                                 oint[:, g * GT + i, kc * KP:kc * KP + KP], t.identb[:])
                    mm.then_inc(oT_ps, 1)
                pe.wait_ge(oT_ready, KC * (g + 1))
                for b in (2 * g, 2 * g + 1):
                    if b >= 2:
                        pe.wait_ge(p_used, b - 1)
                    for i in range(2):
                        tile = 2 * b + i
                        for kc in range(KC):
                            mm = nc.tensor.matmul(psP[:, b % 2, i * D:i * D + D], oT[:, kc, tile * P:tile * P + P],
                                                  t.wpT[:, kc, :], start=(kc == 0), stop=(kc == KC - 1))
                    mm.then_inc(p_ps, 1)
            pe.wait_ge(g_hi_ready, 1)
            pe.wait_ge(g_lo_ready, 2)
            pe.wait_ge(zeros_ready, 1)
            pe.wait_ge(identh_ready, 1)
            for g in range(NG):
                for c in range(XCH):
                    n = XCH * g + c
                    if n >= 2:
                        pe.wait_ge(xT_ready, n - 1)
                    if c == 0:
                        pe.wait_ge(x_hi_ready, g + 1)
                    if c == 3:
                        pe.wait_ge(x_lo_ready, g + 1)
                    for i in range(GT):
                        mm = nc.tensor.transpose(psT[:, n % 2, i * P:i * P + P], xs[:, g * GT + i, c * P:c * P + P], identh[:])
                    mm.then_inc(xT_ps, 1)
                pe.wait_ge(xT_ready, XCH * (g + 1))
                for i in range(GT):
                    tile = g * GT + i
                    for c in range(XCH):
                        mm = nc.tensor.matmul(psG[:, tile * E:tile * E + E], t.xT[:, c, tile * P:tile * P + P],
                                              gparts[:, WEIGHTS_OF[c], :], start=(c == 0), stop=(c == XCH - 1))
                    mm.then_inc(gate_ps, 1)


def experts(nc, t, io):
    with ExitStack() as ctx:
        def sb(name, shape, dt):
            return ctx.enter_context(nc.sbuf_tensor(name, shape, dt))

        def sem(name):
            return ctx.enter_context(nc.semaphore(name))

        W = t.W
        STEPS = 2 * NG
        HSLOTS = 4
        b2r = sb("b2r", [P, E, D], F32)
        hid = sb("hid", [P, HC, GTOK], F32)
        hi = sb("hid_hi", [P, 2, HC, GTOK], F16)
        lo = sb("hid_lo", [P, 2, HC, GTOK], F16)
        part = sb("part", [P, GT, D], F32)
        rank = sb("rank_sb", [P, E], F32)
        prob = sb("prob", [P, NT, E], F32)
        left = sb("left", [P, NT, E], F32)
        pick = sb("pick", [P, 2, NT, E], F32)
        top = sb("top", [P, 3, NT], F32)
        psH = ctx.enter_context(nc.psum_tensor("psH", [P, HSLOTS, 512], F32))
        psE = ctx.enter_context(nc.psum_tensor("psE", [P, GT, 512], F32))
        hid_ps, hid_ready, hi_ready, lo_ready, out_ps, part_ready, added = (
            sem(n) for n in ("hid_ps", "hid_ready", "hi_ready", "lo_ready", "out_ps", "part_ready", "added"))
        bias_in, stored, gelu_starts = sem("f_bias_in"), sem("stored"), sem("gelu_starts")
        gate_step, diff_ready, exp_ready = sem("gate_step"), sem("diff_ready"), sem("exp_ready")
        block = ctx.enter_context(nc.Block())

        def steps(eng, body, lag):
            for s in range(STEPS):
                body(0, s)
            with eng.Fori(1, E // 2 - 1) as i:
                for s in range(STEPS):
                    body(i, s)
            for s in range(STEPS):
                body(E // 2 - 1, s)
            if lag:
                body(E // 2, 0)

        def step_at(i, s, lag):
            row, q = (i, s - lag) if s >= lag else (i - 1, s - lag + STEPS)
            if type(i) is int and not 0 <= row < E // 2:
                return None
            return row, q

        def next_expert(i, s):
            n = i * 2 + (s // NG + 1)
            if type(n) is int and n >= E:
                return None
            return n, (s // NG + 1) % 2, (i if s < NG else i + 1)

        @block.sync
        def _(sp):
            sp.dma_start(b2r[:].rearrange("p e d -> p (e d)"), io.b2.rearrange("e d -> (e d)").partition_broadcast(P)).then_inc(bias_in, 16)

            sp.dma_start(rank[:], io.rank).then_inc(bias_in, 16)

            def load(i, s):
                n = i * 2 + s
                sp.wait_ge(W.hi_ready, n * 2 - 2)
                sp.wait_ge(W.lo_ready, n * 3 - 3)
                load_expert(nc, sp, W, io, n, s)

            with sp.Fori(1, E // 2) as i:
                for s in range(2):
                    load(i, s)
            for g in range(NG):
                sp.wait_ge(added, E * NT - NT + (g + 1) * GT)
                for r in range(g * GT, g * GT + GT):
                    b, c = divmod(r, TB)
                    sp.dma_start(io.out[b, c * P:c * P + P, :], t.h[:, r, :]).then_inc(stored, 16)
            sp.wait_ge(stored, 16 * NT)

        @block.tensor
        def _(pe):
            def hidden(i, s):
                if s % NG == 0:
                    pe.wait_ge(W.lo_ready, (i * 2 + s // NG) * 3 + 3)
                for j in range(HC):
                    n = s * HC + j
                    if n >= HSLOTS or type(i) is not int or i > 0:
                        pe.wait_ge(hid_ready, i * (STEPS * HC) + (n + 1 - HSLOTS))
                    g = s % NG
                    for c in range(XCH):
                        mm = nc.tensor.matmul(psH[:, n % HSLOTS, :], W.w1[:, s // NG, WEIGHTS_OF[c], j * P:j * P + P],
                                              t.xT[:, c, g * GTOK:g * GTOK + GTOK], start=(c == 0), stop=(c == XCH - 1))
                    mm.then_inc(hid_ps, 1)

            def output(i, s):
                pe.wait_ge(hi_ready, i * (STEPS * HC) + (s + 1) * HC)
                pe.wait_ge(lo_ready, i * (STEPS * HC) + (s + 1) * HC)
                for r in range(GT):
                    if s >= 1 or type(i) is not int or i > 0:
                        pe.wait_ge(part_ready, i * (STEPS * GT) + (s * GT + r + 1 - GT))
                    for j in range(HC):
                        for k, (x, w) in enumerate(((hi, 0), (hi, 1), (lo, 0))):
                            mm = nc.tensor.matmul(psE[:, r, 0:D], x[:, s % 2, j, r * P:r * P + P], W.w2[:, s // NG, j, w, :],
                                                  start=(j == 0 and k == 0), stop=(j == HC - 1 and k == 2))
                    mm.then_inc(out_ps, 1)

            def body(i, s):
                if type(i) is not int or i < E // 2:
                    hidden(i, s)
                if at := step_at(i, s, 1):
                    output(*at)

            steps(pe, body, 1)

        @block.gpsimd
        def _(pool):
            def body(i, s):
                if at := next_expert(i, s):
                    n, slot, k = at
                    if s % NG == 0:
                        total_sums_pool(nc, pool, W, n, slot)

            steps(pool, body, 0)

        @block.scalar
        def _(act):
            act.wait_ge(diff_ready, 1)
            nc.scalar.activation(prob[:], left[:], ACT.Exp, scale=t.gundo[:]).then_inc(exp_ready, 1)

            def body(i, s):
                if at := next_expert(i, s):
                    n, slot, k = at
                    if s % NG == 2:
                        if type(i) is not int or i > 0 or s >= NG:
                            act.wait_ge(out_ps, (i * STEPS + (s // NG) * NG) * GT)
                        high_parts_act(nc, act, W, n, slot)
                for j in range(HC):
                    m = s * HC + j
                    if type(i) is not int or i > 0 or s >= 1:
                        act.wait_ge(lo_ready, i * (STEPS * HC) + (m + 1 - HC))
                    act.wait_ge(hid_ps, i * (STEPS * HC) + (m + 1))
                    act.sem_inc(gelu_starts, 1)
                    nc.scalar.activation(hid[:, j, :], psH[:, m % HSLOTS, :], ACT.Gelu, scale=W.undo[:, s // NG, 0:1],
                                         bias=W.b1[:, bass.ds((i * 2 + s // NG) * HC + j, 1)]).then_inc(hid_ready, 1)
                if s % NG == 0 and (at := next_expert(i, s)):
                    square_sums_act(nc, act, W, *at)

            steps(act, body, 0)

        @block.vector
        def _(dve):
            step = chain_on(dve, gate_step)
            def per_token(a):
                return a.unsqueeze(2).broadcast_to([P, NT, E])

            ranks = rank[:].unsqueeze(1).broadcast_to([P, NT, E])
            logits = t.logits[:].rearrange("p (r e) -> p r e", e=E)
            step(nc.vector.tensor_reduce(top[:, 0, :], logits, AX, ALU.max))
            nc.vector.tensor_tensor(left[:], logits, per_token(top[:, 0, :]), ALU.subtract).then_inc(diff_ready, 1)

            def choose_experts():
                dve.wait_ge(exp_ready, 1)
                step(nc.vector.tensor_reduce(top[:, 0, :], prob[:], AX, ALU.add))
                step(nc.vector.reciprocal(top[:, 1, :], top[:, 0, :]))
                step(nc.vector.tensor_tensor(prob[:], prob[:], per_token(top[:, 1, :]), ALU.mult))
                step(nc.vector.tensor_copy(left[:], prob[:]))
                for n in range(2):
                    one = pick[:, n]
                    step(nc.vector.tensor_reduce(top[:, n, :], left[:], AX, ALU.max))
                    step(nc.vector.tensor_tensor(one, left[:], per_token(top[:, n, :]), ALU.is_equal))
                    step(nc.vector.tensor_tensor(one, one, ranks, ALU.mult))
                    step(nc.vector.tensor_reduce(top[:, 2, :], one, AX, ALU.max))
                    step(nc.vector.tensor_tensor(one, one, per_token(top[:, 2, :]), ALU.is_equal))
                    step(nc.vector.scalar_tensor_tensor(out=left[:], in0=one, scalar=-2.0, in1=left[:],
                                                        op0=ALU.mult, op1=ALU.add))
                step(nc.vector.tensor_tensor(top[:, 2, :], top[:, 0, :], top[:, 1, :], ALU.add))
                step(nc.vector.tensor_scalar(top[:, 2, :], top[:, 2, :], 1e-09, None, ALU.add))
                step(nc.vector.reciprocal(top[:, 2, :], top[:, 2, :]))
                step(nc.vector.tensor_tensor(prob[:], prob[:], per_token(top[:, 2, :]), ALU.mult))
                step(nc.vector.tensor_tensor(pick[:, 0], pick[:, 0], pick[:, 1], ALU.add))
                step(nc.vector.tensor_tensor(t.share[:].rearrange("p e r -> p r e"), prob[:], pick[:, 0], ALU.mult))

            dve.wait_ge(bias_in, 32)

            def split(i, s):
                scale = W.mult[:, s // NG, 2:3]
                if type(i) is not int or i > 0 or s >= 2:
                    dve.wait_ge(out_ps, (i * STEPS + (s - 1)) * GT)
                for j in range(HC):
                    m = s * HC + j
                    dve.wait_ge(hid_ready, i * (STEPS * HC) + (m + 1))
                    nc.vector.tensor_scalar(hi[:, s % 2, j, :], hid[:, j, :], scale, None, ALU.mult).then_inc(hi_ready, 1)
                    dve.wait_ge(hi_ready, i * (STEPS * HC) + (m + 1))
                    nc.vector.scalar_tensor_tensor(out=lo[:, s % 2, j, :], in0=hid[:, j, :], scalar=scale,
                                                   in1=hi[:, s % 2, j, :], op0=ALU.mult, op1=ALU.subtract).then_inc(lo_ready, 1)

            def add(i, s):
                e = i * 2 + s // NG
                g = s % NG
                for r in range(GT):
                    dve.wait_ge(out_ps, (i * STEPS + s) * GT + (r + 1))
                    if s >= 1 or type(i) is not int or i > 0:
                        dve.wait_ge(added, i * (STEPS * GT) + (s * GT + r + 1 - GT))
                    nc.vector.scalar_tensor_tensor(out=part[:, r, :].unsqueeze(1), in0=psE[:, r, 0:D].unsqueeze(1),
                                                   scalar=W.undo[:, s // NG, 1:2], in1=b2r[:, bass.ds(e, 1), :],
                                                   op0=ALU.mult, op1=ALU.add).then_inc(part_ready, 1)
                for r in range(GT):
                    dve.wait_ge(part_ready, i * (STEPS * GT) + (s * GT + r + 1))
                    tile = g * GT + r
                    nc.vector.scalar_tensor_tensor(out=t.h[:, tile, :], in0=part[:, r, :],
                                                   scalar=t.share[:].rearrange("p e r -> p (e r)")[:, bass.ds(e * NT + tile, 1)],
                                                   in1=t.h[:, tile, :], op0=ALU.mult, op1=ALU.add).then_inc(added, 1)

            def body(i, s):
                if type(i) is not int or i < E // 2:
                    split(i, s)
                    if type(i) is int and i == 0 and s == 0:
                        choose_experts()
                    if s % NG == 1 and (at := next_expert(i, s)):
                        scales_dve(nc, dve, W, at[0], at[1])
                    if s % NG == 2 and (at := next_expert(i, s)):
                        low_parts_dve(nc, dve, W, at[0], at[1])
                if at := step_at(i, s, 1):
                    add(*at)

            steps(dve, body, 1)


def program(nc, x, mask, token_table, segm_table, w_qkv, b_qkv, w_proj, b_proj, gate_w, w1, b1, w2, b2,
            pos, ident, headmask, rank, out, dump=None):
    io = Inputs()
    io.x, io.mask, io.token_table, io.segm_table = x, mask, token_table, segm_table
    io.w_qkv, io.b_qkv, io.w_proj, io.b_proj, io.gate_w = w_qkv, b_qkv, w_proj, b_proj, gate_w
    io.w1, io.b1, io.w2, io.b2, io.out = w1, b1, w2, b2, out
    io.pos, io.ident, io.headmask, io.rank = pos, ident, headmask, rank
    with ExitStack() as ctx:
        def sb(name, shape, dt):
            return ctx.enter_context(nc.sbuf_tensor(name, shape, dt))

        t = Shared()
        t.h = sb("h", [P, NT, D], F32)
        t.v = sb("v", [P, NT, D], BF16)
        t.o = sb("o", [P, NT, D], F32)
        t.ident = sb("ident_sb", [P, P], F32)
        t.identb = sb("identb", [P, P], BF16)
        t.headmask = sb("headmask_sb", [P, HEADS], F32)
        t.wscale = sb("wscale", [P, WCH + 2], F32)
        t.wpT = sb("wpT", [KP, KC, D], BF16)
        t.yall, t.ypar = sb("yall", [P, 2], F32), sb("ypar", [P, 4], F32)
        t.omax, t.onmin = sb("omax", [P, NT], F32), sb("onmin", [P, NT], F32)
        t.rowmax = sb("rowmax", [P, NT * HEADS], F32)
        t.negc2, t.smpar = sb("negc2", [P, 1], F32), sb("smpar", [P, 6], F32)
        with ExitStack() as qk:
            t.kf = qk.enter_context(nc.sbuf_tensor("kf", [P, 2, TOK], BF16))
            t.qm = qk.enter_context(nc.sbuf_tensor("qm", [P, HEADS, TOK], BF16))
            load_weights_and_tokens(nc, t, io)
            if dump == "A":
                return dump_all(nc, t, out)
            score_extremes(nc, t)
            if dump == "B":
                return dump_all(nc, t, out)
            attention(nc, t)
            if dump == "C":
                return dump_all(nc, t, out)
        t.xT, t.share = sb("xT_parts", [P, XCH, TOK], F16), sb("share", [P, E, NT], F32)
        t.logits, t.gundo = sb("logits", [P, NT * E], F32), sb("gundo", [P, 1], F32)
        t.W = Prepared(sb, lambda name: ctx.enter_context(nc.semaphore(name)))
        project_and_route(nc, t, io)
        if dump == "D":
            return dump_all(nc, t, out)
        experts(nc, t, io)


_INS = ['x', 'mask_BS_i2_0', 'L0_tok_token_table', 'L0_tok_segm_table', 'L0_attn_w_qkv', 'L0_attn_b_qkv',
        'L0_attn_w_proj', 'L0_attn_b_proj', 'L0_ffn_gate_w', 'L0_ffn_w1', 'L0_ffn_b1', 'L0_ffn_w2', 'L0_ffn_b2']
_OUTS = [((B, S, D), 'float32')]


def shape_constants():
    import numpy as np
    f = np.float32
    feature = np.arange(D, dtype=f)
    angle = np.arange(S, dtype=f)[:, None] / np.power(f(10000.0), np.floor(feature / f(2)) * f(2) / f(D))[None, :]
    pos = np.where(np.arange(D) % 2 == 0, np.sin(angle), np.cos(angle)).astype(f)
    headmask = (np.arange(P)[:, None] // HD == np.arange(HEADS)[None, :] % HPC).astype(f)
    rank = np.repeat(np.arange(E, 0, -1, dtype=f)[None, :], P, axis=0)
    return {'pos': pos, 'ident': np.eye(P, dtype=f), 'headmask': headmask, 'rank': rank}


def kernel(**inputs):
    import numpy as _np
    import concourse.bacc as _bacc
    from concourse import mybir as _mybir
    from concourse.bass_utils import run_bass_kernel_spmd as _run

    nc = _bacc.Bacc("TRN2", target_bir_lowering=False, num_devices=1)
    arrays, args = {}, []
    for name, a in [(n, inputs[n]) for n in _INS] + list(shape_constants().items()):
        a = _np.ascontiguousarray(a)
        arrays[f"in_{name}_dram"] = a
        args.append(nc.dram_tensor(f"in_{name}_dram", a.shape, _mybir.dt.from_np(a.dtype), kind="ExternalInput").ap())
    for i, (shape, dtype) in enumerate(_OUTS):
        dt = _mybir.dt.from_np(_np.dtype(dtype))
        args.append(nc.dram_tensor(f"out_{i}_dram", shape, dt, kind="ExternalOutput").ap())
    program(nc, *args)
    r = _run(nc, [arrays], core_ids=[0])
    got = tuple(r.results[0][f"out_{i}_dram"] for i in range(len(_OUTS)))
    return got[0]
```
